# Optimizing a Trainium2 kernel written in Bass

```python
import numpy as np
import jax
import jax.numpy as jnp

def _softmax(x, axis=-1):
    return jax.nn.softmax(x, axis=axis)

def _gelu(x):
    return jax.nn.gelu(x, approximate=True)

def _silu(x):
    return jax.nn.silu(x)

def _sigmoid(x):
    return jax.nn.sigmoid(x)

def _layernorm(x, axis=-1, eps=1e-05):
    m = jnp.mean(x, axis=axis, keepdims=True)
    v = jnp.var(x, axis=axis, keepdims=True)
    return (x - m) / jnp.sqrt(v + eps)

def _scatter_add(tgt, idx, src, axis=0):
    return tgt.at[idx].add(src)

def _segment_sum(src, seg, n):
    return jax.ops.segment_sum(src, seg, n)
kernel_name = 'mk_gnn_resnorm_d1_gnn_r8_4e3f2a'

def setup_inputs(seed: int=0):
    np.random.seed(seed)
    _w = jnp.asarray

    def _rec_inputs():
        import jax
        import jax.numpy as jnp
        _gk = jax.random.key(seed)
        x = -0.0001126 + 1 * jax.random.normal(jax.random.fold_in(_gk, 1), (1250, 768), jnp.float32)
        src = jax.random.randint(jax.random.fold_in(_gk, 2), (20000,), 0, 1250, jnp.int32)
        dst = jax.random.randint(jax.random.fold_in(_gk, 3), (20000,), 0, 1250, jnp.int32)
        _o = jnp.argsort(dst, stable=True)
        src = src[_o]
        dst = dst[_o]
        return (x, src, dst)
    x, src, dst = _rec_inputs()

    def _L0_gnn_setup():
        import jax, jax.numpy as jnp
        import numpy as np
        N_NODES = 1250
        N_EDGES = 20000
        NEG_SLOPE = 0.2

        def _gat_layer(x, src, dst, W, a_src, a_dst, bias, concat):
            N = x.shape[0]
            H, C = a_src.shape
            h = (x @ W).reshape(N, H, C)
            al_s = jnp.einsum('nhc,hc->nh', h, a_src)
            al_d = jnp.einsum('nhc,hc->nh', h, a_dst)
            e = jax.nn.leaky_relu(al_s[src] + al_d[dst], NEG_SLOPE)
            m = jax.ops.segment_max(e, dst, num_segments=N)
            ex = jnp.exp(e - m[dst])
            denom = jax.ops.segment_sum(ex, dst, num_segments=N)
            alpha = ex / (denom[dst] + 1e-16)
            msg = h[src] * alpha[:, :, None]
            out = jax.ops.segment_sum(msg, dst, num_segments=N)
            out = out.reshape(N, H * C) if concat else out.mean(axis=1)
            return out + bias
        key = jax.random.key(seed)
        ks = jax.random.split(key, 10)
        in_dim, hid, out_dim, heads = (768, 512, 768, 4)
        x = jax.random.normal(ks[0], (N_NODES, in_dim), dtype=jnp.float32)
        edge_index = jax.random.randint(ks[1], (2, N_EDGES), 0, N_NODES, dtype=jnp.int64)
        g = lambda k, shape, fan: jax.random.normal(k, shape, jnp.float32) / np.sqrt(fan)
        return {'x': x, 'edge_index': edge_index, 'W1': g(ks[2], (in_dim, heads * hid), in_dim), 'att_src1': g(ks[3], (heads, hid), hid), 'att_dst1': g(ks[4], (heads, hid), hid), 'b1': jnp.zeros((heads * hid,), jnp.float32), 'W2': g(ks[5], (heads * hid, out_dim), heads * hid), 'att_src2': g(ks[6], (1, out_dim), out_dim), 'att_dst2': g(ks[7], (1, out_dim), out_dim), 'b2': jnp.zeros((out_dim,), jnp.float32)}
    _L0_gnn_all = _L0_gnn_setup()
    _L0_gnn_in = {k: v for k, v in _L0_gnn_all.items() if k in ('W1', 'att_src1', 'att_dst1', 'b1', 'W2', 'att_src2', 'att_dst2', 'b2')}
    del _L0_gnn_all
    return {'x': x, 'src': src, 'dst': dst, 'L0_gnn_W1': _L0_gnn_in['W1'], 'L0_gnn_att_src1': _L0_gnn_in['att_src1'], 'L0_gnn_att_dst1': _L0_gnn_in['att_dst1'], 'L0_gnn_b1': _L0_gnn_in['b1'], 'L0_gnn_W2': _L0_gnn_in['W2'], 'L0_gnn_att_src2': _L0_gnn_in['att_src2'], 'L0_gnn_att_dst2': _L0_gnn_in['att_dst2'], 'L0_gnn_b2': _L0_gnn_in['b2']}

def reference(x, src, dst, L0_gnn_W1, L0_gnn_att_src1, L0_gnn_att_dst1, L0_gnn_b1, L0_gnn_W2, L0_gnn_att_src2, L0_gnn_att_dst2, L0_gnn_b2):
    import jax
    import jax.numpy as jnp

    def _L0_gnn_ref(x, edge_index, W1, att_src1, att_dst1, b1, W2, att_src2, att_dst2, b2):
        import jax, jax.numpy as jnp
        import numpy as np
        N_NODES = 1250
        N_EDGES = 20000
        NEG_SLOPE = 0.2

        def _gat_layer(x, src, dst, W, a_src, a_dst, bias, concat):
            N = x.shape[0]
            H, C = a_src.shape
            h = (x @ W).reshape(N, H, C)
            al_s = jnp.einsum('nhc,hc->nh', h, a_src)
            al_d = jnp.einsum('nhc,hc->nh', h, a_dst)
            e = jax.nn.leaky_relu(al_s[src] + al_d[dst], NEG_SLOPE)
            m = jax.ops.segment_max(e, dst, num_segments=N)
            ex = jnp.exp(e - m[dst])
            denom = jax.ops.segment_sum(ex, dst, num_segments=N)
            alpha = ex / (denom[dst] + 1e-16)
            msg = h[src] * alpha[:, :, None]
            out = jax.ops.segment_sum(msg, dst, num_segments=N)
            out = out.reshape(N, H * C) if concat else out.mean(axis=1)
            return out + bias
        N = x.shape[0]
        loops = jnp.arange(N, dtype=edge_index.dtype)
        src = jnp.concatenate([edge_index[0], loops])
        dst = jnp.concatenate([edge_index[1], loops])
        h = jax.nn.elu(_gat_layer(x, src, dst, W1, att_src1, att_dst1, b1, concat=True))
        out = _gat_layer(h, src, dst, W2, att_src2, att_dst2, b2, concat=False)
        return out
    edge_index = jnp.stack([src, dst])
    x = _layernorm(x + _L0_gnn_ref(x, edge_index, L0_gnn_W1, L0_gnn_att_src1, L0_gnn_att_dst1, L0_gnn_b1, L0_gnn_W2, L0_gnn_att_src2, L0_gnn_att_dst2, L0_gnn_b2), axis=-1)
    return x

_drawn_inputs = setup_inputs


def setup_inputs(seed=0):
    import zlib

    import numpy as np

    out = dict(_drawn_inputs(seed))
    spreads = {'L0_gnn_b1': (0.0, 0.1), 'L0_gnn_b2': (0.0, 0.1)}
    factors = {'L0_gnn_att_dst1': 3.66, 'L0_gnn_att_src2': 2.924, 'L0_gnn_att_dst2': 8.0}
    for name, (base, spread) in spreads.items():
        noise = np.random.default_rng([zlib.crc32(name.encode()), seed]).standard_normal(out[name].shape)
        drawn = base * np.exp(spread * noise) if base else spread * noise
        out[name] = jnp.asarray(drawn.astype(out[name].dtype))
    for name, factor in factors.items():
        out[name] = (out[name] * factor).astype(out[name].dtype)
    return out
```

```python
from contextlib import ExitStack

import concourse.bass as bass
from concourse import mybir

F32 = mybir.dt.float32
F32R = mybir.dt.float32r
BF16 = mybir.dt.bfloat16
U16 = mybir.dt.uint16
I32 = mybir.dt.int32
ALU = mybir.AluOpType
ACT = mybir.ActivationFunctionType
AX = mybir.AxisListType
RMAX = bass.bass_isa.ReduceOp.max

N = 1250
E = 20000
B = 125
NB = N // B
PAIRS = E // (2 * B)
D = 768
H = 4
HC = 512
KD = D // 128
HID = H * HC
KC = HID // 128
KH = KC // 2
DH = D // 2
SLOPE = 0.2
EPS = 1e-5
MASKED = -1.0e30
CW = 417
CCH = [(0, CW), (CW, 2 * CW), (2 * CW, N)]
BANK = 512
TCH = [(0, 4), (4, 8), (8, 10)]


def steps(eng, n, front, back, body):
    for j in range(front):
        body(j, j % 2)
    if n - back > front:
        with eng.Fori(front // 2, (n - back) // 2) as k:
            for u in range(2):
                body(2 * k + u, u)
    for j in range(n - back, n):
        body(j, j % 2)


def gat_kernel(nc, x, src, dst, W1, as1, ad1, b1, W2, as2, ad2, b2, out):
    xT_d = nc.dram_tensor("xT_scratch", (NB, 128, 2, KD * B), F32, kind="Internal").ap()
    hid_d = nc.dram_tensor("hidden_scratch", (N, HID), F32, kind="Internal").ap()
    al_d = nc.dram_tensor("scores_scratch", (H, N), F32, kind="Internal").ap()
    al2_d = nc.dram_tensor("scores2_scratch", (1, N), F32, kind="Internal").ap()

    with ExitStack() as ctx:
        def sem(name):
            return ctx.enter_context(nc.semaphore(name))

        cursor = [((nc.sbuf_base + 31) // 32) * 32]
        top = [cursor[0]]

        def sb(name, shape, dt):
            size = 1
            for s in shape[1:]:
                size *= s
            size *= {F32: 4, F32R: 4, I32: 4, BF16: 2, U16: 2}[dt]
            t = nc.alloc_sbuf_tensor_at(name, shape, dt, offset=cursor[0])
            cursor[0] += ((size + 31) // 32) * 32
            top[0] = max(top[0], cursor[0])
            return t

        C = sb("counts", [B, NB, N], U16)
        ident = sb("ident", [128, 128], F32)
        ident_b = sb("ident_b", [128, 128], BF16)
        colid = sb("colid", [B, N], U16)
        rowid = sb("rowid", [B, NB], F32)
        al = sb("al", [B, 2 * H, NB], F32)
        al_rows = sb("al_rows", [H * NB, B], F32)
        negm = sb("negm", [B, (H + 1) * NB], F32)
        rden = sb("rden", [B, (H + 1) * NB], F32)
        mx = sb("mx", [B, 1], F32)
        gate = sb("gate", [B, 1], F32)
        mneg = sb("mneg", [B, 1], F32)
        den = sb("den", [B, 1], F32)
        deps = sb("deps", [B, 1], F32)
        al2 = sb("al2", [B, 2, NB], F32)
        al2_rows = sb("al2_rows", [NB, B], F32)
        bnst = sb("bnst", [B, 2, 6], F32)
        mv = sb("mv", [B, 2], F32)
        vpe = sb("vpe", [B, 1], F32)
        rstd = sb("rstd", [B, NB], F32)
        mhalf = sb("mhalf", [B, 1], F32)
        base0 = cursor[0]

        W1hi = sb("W1hi", [128, KD, HC], F32R)
        W1lo = sb("W1lo", [128, KD, HC], F32R)
        w1raw = sb("w1raw", [128, KD, HC], F32)
        hhi = sb("hhi", [B, NB, HC], F32R)
        hlo = sb("hlo", [B, NB, HC], F32R)
        base1 = cursor[0]

        xahi = sb("xahi", [128, NB, KD, B], F32R)
        xalo = sb("xalo", [128, NB, KD, B], F32R)
        xraw = sb("xraw", [B, 2, D], F32)
        attr = sb("attr", [128, 2 * H, HC], F32)
        oh_src = sb("oh_src", [B, 2, N], BF16)
        oh_dst = sb("oh_dst", [B, 2, B], BF16)
        eye = sb("eye", [B, 2, N], BF16)
        wa_f = sb("wa_f", [128, KD, 2 * H], F32)
        wahi = sb("wahi", [128, KD, 2 * H], F32R)
        walo = sb("walo", [128, KD, 2 * H], F32R)
        junk_w = sb("junk_w", [128, 2, HC], BF16)
        dst_i = sb("dst_i", [PAIRS, 2, B], I32)
        src_i = sb("src_i", [PAIRS, 2, B], I32)
        dst_f = sb("dst_f", [PAIRS, 2, B], F32)
        src_f = sb("src_f", [PAIRS, 2, B], F32)
        ecol = sb("ecol", [B, 4, PAIRS], F32)
        blk_lo = sb("blk_lo", [PAIRS, NB], F32)
        blk_hi = sb("blk_hi", [PAIRS, NB], F32)
        pairid = sb("pairid", [PAIRS, 1], F32)
        pairrv = sb("pairrv", [PAIRS, 1], F32)
        dmin = sb("dmin", [PAIRS, 1], F32)
        dmax = sb("dmax", [PAIRS, 1], F32)
        hit = sb("hit", [PAIRS, 3, NB], F32)
        key = sb("key", [PAIRS, 2 * NB], F32)
        keyr = sb("keyr", [PAIRS, 2 * NB], F32)
        rng_f = sb("rng_f", [1, 5, NB], F32)
        rng_i = sb("rng_i", [1, 5, NB], I32)
        ones1 = sb("ones1", [1, NB], F32)

        cursor[0] = base1
        prow = sb("prow", [B, 2, N], F32)
        PThi = sb("PThi", [B, 2, NB, B], F32R)
        PTlo = sb("PTlo", [B, 2, NB, B], F32R)
        xr = sb("xr", [128, 2, 2, KD * B], F32R)
        b1row = sb("b1row", [B, HID], F32)
        vbuf = sb("vbuf", [B, 2, HC], F32)
        ebuf = sb("ebuf", [B, 2, HC], F32)
        nbr = sb("nbr", [B, N], BF16)
        junk = sb("junk", [B, N], BF16)
        arow = sb("arow", [B, H, N], F32)

        cursor[0] = base0
        W2hi = sb("W2hi", [128, KC, D], F32R)
        W2lo = sb("W2lo", [128, KC, D], F32R)
        h2f = sb("h2f", [B, NB, D], F32)
        hThi = sb("hThi", [128, 2, KH, B], F32R)
        hTlo = sb("hTlo", [128, 2, KH, B], F32R)
        hblk = sb("hblk", [B, 2, HID], F32)
        a2row = sb("a2row", [B, 2, D], F32)
        w2raw = sb("w2raw", [128, 3, D], F32)
        a2junk = sb("a2junk", [B, 2, D], BF16)

        cursor[0] = base0
        h2hi = sb("h2hi", [B, NB, D], F32R)
        h2lo = sb("h2lo", [B, NB, D], F32R)
        prow2 = sb("prow2", [B, 2, N], F32)
        PT2hi = sb("PT2hi", [B, 2, NB, B], F32R)
        PT2lo = sb("PT2lo", [B, 2, NB, B], F32R)
        arow2 = sb("arow2", [B, 1, N], F32)
        assert cursor[0] <= base0 + 2 * KC * D * 4
        cursor[0] = base0 + 2 * KC * D * 4 + NB * D * 4
        y = sb("y", [B, NB, D], F32)
        b2row = sb("b2row", [B, D], F32)
        xres = sb("xres", [B, 2, D], F32)
        nbr2 = sb("nbr2", [B, N], BF16)
        junk2 = sb("junk2", [B, N], BF16)
        assert top[0] <= nc.sbuf_usable_end, (top[0], nc.sbuf_usable_end)

        PS = ctx.enter_context(nc.psum_tensor("ps", [128, 8, BANK], F32))

        ld_edges = sem("ld_edges")
        ld_x = [sem(f"ld_x{i}") for i in range(2)]
        ld_w1 = sem("ld_w1")
        ld_att = sem("ld_att")
        ld_wk = [sem(f"ld_wk{i}") for i in range(3)]
        xT_stored = sem("xT_stored")
        al_stored = sem("al_stored")
        ld_arow = sem("ld_arow")
        ld_b1 = sem("ld_b1")
        ld_xr = [sem(f"ld_xr{i}") for i in range(2)]
        hid_stored = [sem(f"hid_stored{i}") for i in range(2)]
        ld_hb = [sem(f"ld_hb{i}") for i in range(2)]
        ld_a2 = sem("ld_a2")
        ld_w2 = [sem(f"ld_w2{i}") for i in range(3)]
        al2_stored = sem("al2_stored")
        ld_arow2 = sem("ld_arow2")
        ld_b2 = sem("ld_b2")
        ld_xres = [sem(f"ld_xres{i}") for i in range(2)]
        out_stored = sem("out_stored")

        consts = sem("consts")
        consts_v = sem("consts_v")
        edges_f = sem("edges_f")
        ecol_ps = sem("ecol_ps")
        ecol_sb = sem("ecol_sb")
        plan = sem("plan")
        keys_red = sem("keys_red")
        ranges = sem("ranges")
        xt_ps = sem("xt_ps")
        xt_hi = sem("xt_hi")
        xt_lo = sem("xt_lo")
        w1_hi = sem("w1_hi")
        w1_lo = sem("w1_lo")
        h_hi = sem("h_hi")
        h_lo = sem("h_lo")
        mm_done = sem("mm_done")
        wa_done = sem("wa_done")
        wa_hi = sem("wa_hi")
        wa_lo = sem("wa_lo")
        eye_done = sem("eye_done")
        oh_done = sem("oh_done")
        oh_free = sem("oh_free")
        c_done = sem("c_done")
        al_ps = sem("al_ps")
        al_sb = sem("al_sb")
        alr_ps = sem("alr_ps")
        alr_sb = sem("alr_sb")
        m_nb = sem("m_nb")
        m_max = sem("m_max")
        m_neg = sem("m_neg")
        m_done = sem("m_done")
        z_done = sem("z_done")
        e_done = sem("e_done")
        p_done = sem("p_done")
        pc_done = sem("pc_done")
        d_eps = sem("d_eps")
        d_done = sem("d_done")
        t_done = sem("t_done")
        pt_hi = sem("pt_hi")
        pt_lo = sem("pt_lo")
        v_done = sem("v_done")
        ex_done = sem("ex_done")
        r_done = sem("r_done")
        hid_done = sem("hid_done")
        w2_hi = sem("w2_hi")
        w2_lo = sem("w2_lo")
        ht_ps = sem("ht_ps")
        ht_hi = sem("ht_hi")
        ht_lo = sem("ht_lo")
        h2_ps = sem("h2_ps")
        h2_sb = sem("h2_sb")
        al2_done = sem("al2_done")
        al2r_ps = sem("al2r_ps")
        al2r_sb = sem("al2r_sb")
        h2_hi = sem("h2_hi")
        h2_lo = sem("h2_lo")
        mm2_done = sem("mm2_done")
        y_b = sem("y_b")
        y_x = sem("y_x")
        y_st = sem("y_st")
        y_mv = sem("y_mv")
        y_var = sem("y_var")
        y_pow = sem("y_pow")
        y_done = sem("y_done")

        def count_bank(s, c):
            return PS[0:B, 2 + 3 * s + c, 0:CCH[c][1] - CCH[c][0]]

        block = ctx.enter_context(nc.Block())

        @block.sync
        def _(sp):
            sp.dma_start(dst_i[:], dst.rearrange("(p u e) -> p u e", u=2, e=B)).then_inc(ld_edges, 16)
            sp.dma_start(src_i[:], src.rearrange("(p u e) -> p u e", u=2, e=B)).then_inc(ld_edges, 16)

            def load_x(j, s):
                if not (isinstance(j, int) and j < 2):
                    sp.wait_ge(xt_ps, j - 1)
                sp.dma_start(xraw[:, s, :], x[bass.ds(j * B, B), :]).then_inc(ld_x[s], 16)

            def load_w1(h):
                sp.dma_start(w1raw[:], W1[:, h * HC:(h + 1) * HC].rearrange("(k p) c -> p k c", p=128)
                             ).then_inc(ld_w1, 16)

            load_x(0, 0)
            load_x(1, 1)
            load_w1(0)
            sp.dma_start(attr[:, 0:H, :], as1.rearrange("(o h) c -> o h c", o=1).broadcast_to([128, H, HC])
                         ).then_inc(ld_att, 16)
            sp.dma_start(attr[:, H:2 * H, :], ad1.rearrange("(o h) c -> o h c", o=1).broadcast_to([128, H, HC])
                         ).then_inc(ld_att, 16)
            with sp.Fori(1, NB // 2) as k:
                for u in range(2):
                    load_x(2 * k + u, u)

            def store_xT(j, s):
                sp.wait_ge(xt_hi, j + 1)
                sp.wait_ge(xt_lo, j + 1)
                sp.dma_start(xT_d[bass.ds(j, 1), :, 0, :].rearrange("o p n -> p o n"),
                             xahi[:, bass.ds(j, 1), :, :].bitcast(F32).rearrange("p o k n -> p o (k n)")).then_inc(xT_stored, 16)
                sp.dma_start(xT_d[bass.ds(j, 1), :, 1, :].rearrange("o p n -> p o n"),
                             xalo[:, bass.ds(j, 1), :, :].bitcast(F32).rearrange("p o k n -> p o (k n)")).then_inc(xT_stored, 16)
            steps(sp, NB, 0, 0, store_xT)

            sp.wait_ge(w1_hi, KD)
            sp.wait_ge(w1_lo, KD)
            for n in range(2 * KD):
                if n >= 3:
                    sp.wait_ge(wa_done, H * (n - 2))
                sp.dma_start(w1raw[:, 2 * (n % 3):2 * (n % 3) + 2, :],
                             W1[128 * (n // 2):128 * (n // 2) + 128, bass.ts(n % 2, 2 * HC)]
                             .rearrange("p (a c) -> p a c", a=2)).then_inc(ld_wk[n % 3], 16)
            sp.wait_ge(wa_done, 2 * H * KD)
            load_w1(1)

            sp.wait_ge(alr_sb, 1)
            sp.dma_start(al_d.rearrange("h (b p) -> (h b) p", p=B), al_rows[:]).then_inc(al_stored, 16)
            sp.wait_ge(al_stored, 16)
            sp.dma_start(b1row[:], b1.rearrange("(o n) -> o n", o=1).broadcast_to([B, HID])).then_inc(ld_b1, 16)
            for h in range(H):
                sp.dma_start(arow[:, h, :], al_d[h:h + 1, :].broadcast_to([B, N])).then_inc(ld_arow, 16)
                sp.wait_ge(ld_arow, 16 * (h + 1))
            sp.wait_ge(xT_stored, 32 * NB)

            def load_xr(h, j, s):
                if not (h == 1 and isinstance(j, int) and j < 2):
                    sp.wait_ge(mm_done, slot_free(h, j))
                sp.dma_start(xr[:, s, :, :].bitcast(F32), xT_d[bass.ds(j, 1), :, :, :].rearrange("o p t n -> p (o t) n")
                             ).then_inc(ld_xr[s], 16)

            def slot_free(h, j):
                if isinstance(j, int) and j < 2:
                    return 20 * (h - 1) + NB - 2 + j + 1
                return 20 * h + j - 1

            def store_hid(h, j, s):
                sp.wait_ge(hid_done, NB * h + j + 1)
                sp.dma_start(hid_d[bass.ds(j * B, B), h * HC:(h + 1) * HC], ebuf[:, s, :]).then_inc(hid_stored[s], 16)

            for h in range(H):
                if h + 1 < H:
                    load_xr(h + 1, 0, 0)
                    load_xr(h + 1, 1, 1)
                steps(sp, NB, 0, 0, lambda j, s: store_hid(h, j, s))
                if h + 2 < H:
                    sp.wait_ge(w1_hi, KD * (h + 2))
                    sp.wait_ge(w1_lo, KD * (h + 2))
                    load_w1(h + 2)
                if h + 1 < H:
                    with sp.Fori(1, NB // 2) as k:
                        for u in range(2):
                            load_xr(h + 1, 2 * k + u, u)

            sp.wait_ge(mm_done, 2 * H * NB)
            sp.wait_ge(v_done, H * NB)
            for i in range(2):
                sp.wait_ge(hid_stored[i], 16 * H * NB // 2)

            def load_w2(c):
                if c >= 3:
                    sp.wait_ge(w2_hi, c - 2)
                    sp.wait_ge(w2_lo, c - 2)
                sp.dma_start(w2raw[:, c % 3, :], W2[128 * c:128 * c + 128, :]).then_inc(ld_w2[c % 3], 16)

            def load_hb(b, s):
                if not (isinstance(b, int) and b < 2):
                    sp.wait_ge(ht_ps, 2 * b - 2)
                sp.dma_start(hblk[:, s, :], hid_d[bass.ds(b * B, B), :]).then_inc(ld_hb[s], 16)

            load_hb(0, 0)
            for c in range(3):
                load_w2(c)
            load_hb(1, 1)
            sp.dma_start(a2row[:, 0, :], as2.broadcast_to([B, D])).then_inc(ld_a2, 16)
            sp.dma_start(a2row[:, 1, :], ad2.broadcast_to([B, D])).then_inc(ld_a2, 16)
            for c in range(3, KC):
                load_w2(c)
            with sp.Fori(1, NB // 2) as k:
                for u in range(2):
                    load_hb(2 * k + u, u)

            sp.wait_ge(al2r_sb, 1)
            sp.dma_start(al2_d.rearrange("o (b p) -> (o b) p", p=B), al2_rows[:]).then_inc(al2_stored, 16)
            sp.wait_ge(al2_stored, 16)
            sp.dma_start(arow2[:, 0, :], al2_d.broadcast_to([B, N])).then_inc(ld_arow2, 16)
            sp.dma_start(b2row[:], b2.rearrange("(o n) -> o n", o=1).broadcast_to([B, D])).then_inc(ld_b2, 16)

            def load_xres(b, s):
                if not (isinstance(b, int) and b < 2):
                    sp.wait_ge(y_x, b - 1)
                sp.dma_start(xres[:, s, :], x[bass.ds(b * B, B), :]).then_inc(ld_xres[s], 16)

            def store_out(b, s):
                sp.wait_ge(y_done, b + 1)
                sp.dma_start(out[bass.ds(b * B, B), :], y[:, bass.ds(b, 1), :].rearrange("p o n -> p (o n)")
                             ).then_inc(out_stored, 16)

            load_xres(0, 0)
            load_xres(1, 1)
            with sp.Fori(1, NB // 2) as k:
                for u in range(2):
                    load_xres(2 * k + u, u)
                    store_out(2 * k + u - 2, u)
            store_out(NB - 2, 0)
            store_out(NB - 1, 1)
            sp.wait_ge(out_stored, 16 * NB)

        @block.gpsimd
        def _(pool):
            pool.memset(ident[:], 0.0).then_inc(consts, 1)
            pool.iota(colid[:], [[1, N]], base=0, channel_multiplier=0).then_inc(consts, 1)
            pool.iota(rowid[:], [[B, NB]], base=0, channel_multiplier=1,
                      allow_small_or_imprecise_dtypes=True).then_inc(consts, 1)
            pool.iota(blk_lo[:], [[B, NB]], base=0, channel_multiplier=0,
                      allow_small_or_imprecise_dtypes=True).then_inc(consts, 1)
            pool.iota(blk_hi[:], [[B, NB]], base=B, channel_multiplier=0,
                      allow_small_or_imprecise_dtypes=True).then_inc(consts, 1)
            pool.iota(pairid[:], [[1, 1]], base=1, channel_multiplier=1,
                      allow_small_or_imprecise_dtypes=True).then_inc(consts, 1)
            pool.iota(pairrv[:], [[1, 1]], base=PAIRS, channel_multiplier=-1,
                      allow_small_or_imprecise_dtypes=True).then_inc(consts, 1)
            pool.wait_ge(consts, 7)
            pool.affine_select(out=ident[:], in_=ident[:], compare_op=ALU.not_equal, fill=1.0, base=0,
                               pattern=[[-1, 128]], channel_multiplier=1).then_inc(consts, 1)
            pool.wait_ge(plan, 6)
            pool.partition_all_reduce(keyr[:], key[:], PAIRS, RMAX).then_inc(keys_red, 1)

            def split_w1(h, k):
                pool.wait_ge(w1_hi, KD * h + k + 1)
                pool.tensor_tensor(W1lo[:, bass.ds(k, 1), :], w1raw[:, bass.ds(k, 1), :],
                                   W1hi[:, bass.ds(k, 1), :].bitcast(F32), ALU.subtract).then_inc(w1_lo, 1)

            for k in range(KD):
                split_w1(0, k)

            for h in range(1, H):
                steps(pool, KD, 0, 0, lambda k, s: split_w1(h, k))

            def pow_var(b, s):
                pool.wait_ge(y_var, b + 1)
                pool.tensor_tensor(rstd[:, bass.ds(b, 1)], vpe[:], mhalf[:], ALU.pow).then_inc(y_pow, 1)
            steps(pool, NB, 0, 0, pow_var)

        def act_scores(act, g, b, h, s, buf, rows, dcol):
            act.activation(buf[:, s, :], rows[:, h, :], ACT.Identity, bias=dcol).then_inc(z_done, 1)

        def act_exp(act, g, s, buf):
            act.wait_ge(e_done, g + 1)
            act.wait_ge(m_done, g + 1)
            act.activation(buf[:, s, :], buf[:, s, :], ACT.Exp, bias=negm[:, bass.ds(g, 1)]).then_inc(p_done, 1)

        def act_split(act, g, s, hi):
            act.wait_ge(t_done, g + 1)
            act.activation(hi[:, s, 0:8, :].rearrange("p (a b) n -> p a (b n)", a=2),
                           PS[0:B, 2:4, 0:4 * B], ACT.Copy)
            act.activation(hi[:, s, 8:10, :].rearrange("p b n -> p (b n)"),
                           PS[0:B, 4, 0:2 * B], ACT.Copy).then_inc(pt_hi, 1)

        def dve_max(dve, g, b, row, scr, jnk, dcol):
            dve.tensor_scalar(scr[:], C[:, bass.ds(b, 1), :].rearrange("p o n -> p (o n)"), 0.0, MASKED,
                              ALU.is_equal, ALU.mult).then_inc(m_nb, 1)
            dve.wait_ge(m_nb, g + 1)
            dve.memset(gate[:], 0.0)
            dve.tensor_tensor_reduce(out=jnk[:], in0=scr[:], in1=row, scale=1.0, scalar=-3.0e38,
                                     op0=ALU.add, op1=ALU.max, accum_out=mx[:]).then_inc(m_max, 1)
            dve.wait_ge(m_max, g + 1)
            dve.scalar_tensor_tensor(mneg[:], mx[:], -1.0, dcol, ALU.mult, ALU.subtract).then_inc(m_neg, 1)
            dve.wait_ge(m_neg, g + 1)
            dve.scalar_tensor_tensor(negm[:, bass.ds(g, 1)], mneg[:], SLOPE, mneg[:], ALU.mult, ALU.min
                                     ).then_inc(m_done, 1)

        def dve_leaky(dve, g, s, buf):
            dve.wait_ge(z_done, g + 1)
            dve.scalar_tensor_tensor(buf[:, s, :], buf[:, s, :], SLOPE, buf[:, s, :], ALU.mult, ALU.max
                                     ).then_inc(e_done, 1)

        def dve_counts(dve, g, b, s, buf):
            dve.wait_ge(p_done, g + 1)
            dve.scalar_tensor_tensor(buf[:, s, :], buf[:, s, :], 1.0,
                                     C[:, bass.ds(b, 1), :].rearrange("p o n -> p (o n)"),
                                     ALU.min, ALU.mult, accum_out=den[:]).then_inc(pc_done, 1)
            dve.wait_ge(pc_done, g + 1)
            dve.tensor_scalar(deps[:], den[:], 1e-16, None, ALU.add).then_inc(d_eps, 1)
            dve.wait_ge(d_eps, g + 1)
            dve.reciprocal(rden[:, bass.ds(g, 1)], deps[:]).then_inc(d_done, 1)

        def dve_split(dve, g, s, hi, lo):
            dve.wait_ge(pt_hi, g + 1)
            dve.tensor_tensor(lo[:, s, 0:8, :].rearrange("p (a b) n -> p a (b n)", a=2), PS[0:B, 2:4, 0:4 * B],
                              hi[:, s, 0:8, :].bitcast(F32).rearrange("p (a b) n -> p a (b n)", a=2), ALU.subtract)
            dve.tensor_tensor(lo[:, s, 8:10, :].rearrange("p b n -> p (b n)"), PS[0:B, 4, 0:2 * B],
                              hi[:, s, 8:10, :].bitcast(F32).rearrange("p b n -> p (b n)"), ALU.subtract
                              ).then_inc(pt_lo, 1)

        def pe_transpose(pe, g, s, buf):
            for bank, (lo, hi) in enumerate(TCH):
                for b in range(lo, hi):
                    t = pe.transpose(PS[0:B, 2 + bank, (b - lo) * B:(b - lo + 1) * B],
                                     buf[:, s, b * B:(b + 1) * B], ident[0:B, 0:B])
            t.then_inc(t_done, 1)

        @block.scalar
        def _(act):
            def split_xT(j, s):
                act.wait_ge(xt_ps, j + 1)
                act.activation(xahi[:, bass.ds(j, 1), 0:4, :].rearrange("p o k n -> p (o k n)"),
                               PS[:, 2 + 2 * s, 0:4 * B], ACT.Copy)
                act.activation(xahi[:, bass.ds(j, 1), 4:6, :].rearrange("p o k n -> p (o k n)"),
                               PS[:, 3 + 2 * s, 0:2 * B], ACT.Copy).then_inc(xt_hi, 1)

            def split_w1(k):
                act.activation(W1hi[:, bass.ds(k, 1), :], w1raw[:, bass.ds(k, 1), :], ACT.Copy).then_inc(w1_hi, 1)

            def split_h(h, j, s):
                act.wait_ge(mm_done, 2 * NB * h + j + 1)
                act.activation(hhi[:, bass.ds(j, 1), :].rearrange("p o c -> p (o c)"), PS[0:B, s, :], ACT.Copy
                               ).then_inc(h_hi, 1)

            split_xT(0, 0)
            act.wait_ge(ld_w1, 16)
            for k in range(KD):
                split_w1(k)
            split_xT(1, 1)
            with act.Fori(1, NB // 2) as k:
                for u in range(2):
                    split_xT(2 * k + u, u)
            steps(act, NB, 0, 0, lambda j, s: split_h(0, j, s))

            act.wait_ge(wa_done, 2 * H * KD)
            act.activation(wahi[:], wa_f[:], ACT.Copy).then_inc(wa_hi, 1)

            act.wait_ge(ranges, 1)

            def counts_out(b, s):
                last = act.value_load(rng_i[0:1, 4, bass.ds(b, 1)], min_val=4, max_val=2 * NB * PAIRS + 2)
                act.wait_ge(oh_free, last)
                row = C[:, bass.ds(b, 1), :].rearrange("p o n -> p (o n)")
                act.activation(row[:, 0:2 * CW].rearrange("p (a n) -> p a n", a=2),
                               PS[0:B, 2 + 3 * s:4 + 3 * s, 0:CW], ACT.Copy)
                act.activation(row[:, 2 * CW:N], count_bank(s, 2), ACT.Copy).then_inc(c_done, 1)
            steps(act, NB, 0, 0, counts_out)

            def scores(h, b, s):
                act_scores(act, NB * h + b, b, h, s, prow, arow, al[:, H + h, bass.ds(b, 1)])

            act.wait_ge(ld_arow, 16 * H)
            scores(0, 0, 0)
            scores(0, 1, 1)
            act_exp(act, 0, 0, prow)
            act_exp(act, 1, 1, prow)
            act_split(act, 0, 0, PThi)
            scores(0, 2, 0)
            act_exp(act, 2, 0, prow)
            act_split(act, 1, 1, PThi)
            scores(0, 3, 1)

            for h in range(H):
                def step(j, s):
                    g = NB * h + j
                    more = lambda n: not (h == H - 1 and isinstance(j, int) and j + n >= NB)
                    nxt = lambda n: (h + 1, j + n - NB) if isinstance(j, int) and j + n >= NB else (h, j + n)
                    if more(3):
                        act_exp(act, g + 3, 1 - s, prow)
                    last = isinstance(j, int) and j == NB - 1
                    if more(2) and not last:
                        act.wait_ge(mm_done, 2 * NB * h + NB + j + 1)
                        act_split(act, g + 2, s, PThi)
                    act.wait_ge(v_done, g + 1)
                    if not (isinstance(j, int) and j < 2 and h == 0):
                        act.wait_ge(hid_stored[s], stored(h, j, s))
                    act.activation(ebuf[:, s, :], vbuf[:, s, :], ACT.Exp).then_inc(ex_done, 1)
                    if h + 1 < H and not (isinstance(j, int) and j >= KD):
                        split_w1_of(h + 1, j)
                    if more(4) and not last:
                        act.wait_ge(t_done, g + 3)
                        scores(nxt(4)[0], nxt(4)[1], s)

                def stored(h, j, s):
                    return 16 * (NB // 2) * h + 8 * (j - s)

                def split_w1_of(h1, k):
                    if isinstance(k, int) and k == 0:
                        act.wait_ge(ld_w1, 16 * (h1 + 1))
                        act.wait_ge(mm_done, 2 * NB * (h1 - 1) + NB)
                    split_w1(k)
                steps(act, NB, 2, 4, step)
                if h + 1 < H:
                    steps(act, NB, 0, 0, lambda j, s: split_h(h + 1, j, s))
                    act_split(act, NB * (h + 1) + 1, 1, PThi)
                    scores(h + 1, 3, 1)

            def split_hT(n, b, half):
                if not (isinstance(b, int) and b == 0):
                    act.wait_ge(h2_ps, n - 1)
                act.wait_ge(ht_ps, n + 1)
                act.activation(hThi[:, half, :, :].rearrange("p (a k) n -> p a (k n)", a=2),
                               PS[:, 4 + 2 * half:6 + 2 * half, 0:4 * B], ACT.Copy).then_inc(ht_hi, 1)

            def h2_out(b, s):
                act.wait_ge(h2_ps, 2 * b + 2)
                act.activation(h2f[:, bass.ds(b, 1), :].rearrange("p o (a n) -> p (o a) n", a=2),
                               PS[0:B, 2 * s:2 * s + 2, 0:DH], ACT.Copy).then_inc(h2_sb, 1)

            split_hT(0, 0, 0)
            for c in range(KC):
                act.wait_ge(ld_w2[c % 3], 16 * (c // 3 + 1))
                act.activation(W2hi[:, c, :], w2raw[:, c % 3, :], ACT.Copy).then_inc(w2_hi, 1)
                if c == 2:
                    split_hT(1, 0, 1)

            def h2_step(b, s):
                split_hT(2 * b + 2, b + 1, 0)
                split_hT(2 * b + 3, b + 1, 1)
                h2_out(b, s)
            steps(act, NB, 2, 2, lambda b, s: h2_step(b, s) if not (isinstance(b, int) and b == NB - 1) else h2_out(b, s))

            act.wait_ge(h2_ps, 2 * NB)
            act.wait_ge(h2_sb, NB)

            def split_h2(b, s):
                act.activation(h2hi[:, bass.ds(b, 1), :], h2f[:, bass.ds(b, 1), :], ACT.Copy).then_inc(h2_hi, 1)

            def scores2(b, s):
                act_scores(act, G2 + b, b, 0, s, prow2, arow2, al2[:, 1, bass.ds(b, 1)])
            G2 = H * NB
            split_h2(0, 0)
            split_h2(1, 1)
            act.wait_ge(ld_arow2, 16)
            scores2(0, 0)
            scores2(1, 1)
            act_exp(act, G2, 0, prow2)
            act_exp(act, G2 + 1, 1, prow2)
            act_split(act, G2, 0, PT2hi)
            with act.Fori(1, NB // 2) as k:
                for u in range(2):
                    split_h2(2 * k + u, u)
            scores2(2, 0)
            act_exp(act, G2 + 2, 0, prow2)
            act_split(act, G2 + 1, 1, PT2hi)
            scores2(3, 1)

            def step2(j, s):
                g = G2 + j
                more = lambda n: not (isinstance(j, int) and j + n >= NB)
                if more(3):
                    act_exp(act, g + 3, 1 - s, prow2)
                if more(2):
                    act.wait_ge(mm2_done, j + 1)
                    act_split(act, g + 2, s, PT2hi)
                if more(4):
                    act.wait_ge(t_done, g + 3)
                    scores2(j + 4, s)
            steps(act, NB, 0, 4, step2)

        @block.vector
        def _(dve):
            dve.memset(mhalf[:], -0.5).then_inc(consts_v, 1)
            dve.memset(ones1[:], 1.0).then_inc(consts_v, 1)
            dve.wait_ge(ld_edges, 32)
            dve.tensor_copy(dst_f[:], dst_i[:]).then_inc(edges_f, 1)
            dve.tensor_copy(src_f[:], src_i[:]).then_inc(edges_f, 1)
            dve.wait_ge(edges_f, 1)
            dve.tensor_reduce(dmin[:], dst_f[:].rearrange("p u e -> p (u e)"), AX.X, ALU.min).then_inc(plan, 1)
            dve.tensor_reduce(dmax[:], dst_f[:].rearrange("p u e -> p (u e)"), AX.X, ALU.max).then_inc(plan, 1)
            dve.wait_ge(consts, 8)
            dve.wait_ge(plan, 2)
            dve.tensor_scalar(hit[:, 0, :], blk_hi[:], dmin[:], None, ALU.is_gt)
            dve.tensor_scalar(hit[:, 1, :], blk_lo[:], dmax[:], None, ALU.is_le).then_inc(plan, 1)
            dve.wait_ge(plan, 3)
            dve.tensor_tensor(hit[:, 2, :], hit[:, 0, :], hit[:, 1, :], ALU.mult).then_inc(plan, 1)
            dve.wait_ge(plan, 4)
            dve.tensor_scalar(key[:, 0:NB], hit[:, 2, :], pairid[:], None, ALU.mult).then_inc(plan, 1)
            dve.tensor_scalar(key[:, NB:2 * NB], hit[:, 2, :], pairrv[:], None, ALU.mult).then_inc(plan, 1)
            dve.tensor_copy(ident_b[:], ident[:]).then_inc(consts_v, 1)
            dve.wait_ge(ecol_ps, 1)
            dve.tensor_copy(ecol[:].rearrange("p a n -> p (a n)"), PS[0:B, 7, 0:4 * PAIRS]).then_inc(ecol_sb, 1)
            dve.wait_ge(keys_red, 1)
            dve.tensor_scalar(rng_f[:, 3, :], keyr[0:1, NB:2 * NB], -1.0, float(PAIRS), ALU.mult, ALU.add
                              ).then_inc(plan, 1)
            dve.wait_ge(plan, 7)
            dve.tensor_scalar(rng_f[:, 0, :], rng_f[:, 3, :], float(PAIRS - 1), None, ALU.min)
            dve.tensor_tensor(rng_f[:, 1, :], keyr[0:1, 0:NB], rng_f[:, 3, :], ALU.subtract).then_inc(plan, 1)
            dve.wait_ge(plan, 8)
            dve.tensor_scalar(rng_f[:, 1, :], rng_f[:, 1, :], 1.0, None, ALU.max).then_inc(plan, 1)
            dve.wait_ge(plan, 9)
            dve.wait_ge(consts_v, 3)
            dve.tensor_tensor_scan(rng_f[:, 3, :], ones1[:], rng_f[:, 1, :], 0.0, ALU.mult, ALU.add
                                   ).then_inc(plan, 1)
            dve.wait_ge(plan, 10)
            dve.tensor_tensor(rng_f[:, 2, :], rng_f[:, 3, :], rng_f[:, 1, :], ALU.subtract)
            dve.tensor_scalar(rng_f[:, 4, :], rng_f[:, 3, :], 2.0, 2.0, ALU.mult, ALU.add).then_inc(plan, 1)
            dve.wait_ge(plan, 11)
            dve.tensor_copy(rng_i[:], rng_f[:]).then_inc(ranges, 1)

            def split_xT(j, s):
                dve.wait_ge(xt_hi, j + 1)
                dve.tensor_tensor(xalo[:, bass.ds(j, 1), 0:4, :].rearrange("p o k n -> p (o k n)"),
                                  PS[:, 2 + 2 * s, 0:4 * B],
                                  xahi[:, bass.ds(j, 1), 0:4, :].bitcast(F32).rearrange("p o k n -> p (o k n)"),
                                  ALU.subtract)
                dve.tensor_tensor(xalo[:, bass.ds(j, 1), 4:6, :].rearrange("p o k n -> p (o k n)"),
                                  PS[:, 3 + 2 * s, 0:2 * B],
                                  xahi[:, bass.ds(j, 1), 4:6, :].bitcast(F32).rearrange("p o k n -> p (o k n)"),
                                  ALU.subtract).then_inc(xt_lo, 1)
            steps(dve, NB, 0, 0, split_xT)

            def split_h(h, j, s):
                dve.wait_ge(h_hi, NB * h + j + 1)
                dve.tensor_tensor(hlo[:, bass.ds(j, 1), :].rearrange("p o c -> p (o c)"), PS[0:B, s, :],
                                  hhi[:, bass.ds(j, 1), :].bitcast(F32).rearrange("p o c -> p (o c)"),
                                  ALU.subtract).then_inc(h_lo, 1)

            dve.wait_ge(ld_att, 32)

            def fold(n):
                k, half = n // 2, n % 2
                dve.wait_ge(ld_wk[n % 3], 16 * (n // 3 + 1))
                for i, v in enumerate((2 * half, H + 2 * half, 2 * half + 1, H + 2 * half + 1)):
                        hh = i // 2
                        if 4 * n + i >= 2:
                            dve.wait_ge(wa_done, 4 * n + i - 1)
                        dve.tensor_tensor_reduce(out=junk_w[:, i % 2, :], in0=w1raw[:, 2 * (n % 3) + hh, :], in1=attr[:, v, :],
                                                 scale=1.0, scalar=0.0, op0=ALU.mult, op1=ALU.add,
                                                 accum_out=wa_f[:, k, v:v + 1]).then_inc(wa_done, 1)
            for j in range(NB):
                split_h(0, j, j % 2)
                fold(j)
            fold(NB)
            fold(NB + 1)
            dve.wait_ge(wa_hi, 1)
            dve.tensor_tensor(walo[:], wa_f[:], wahi[:].bitcast(F32), ALU.subtract).then_inc(wa_lo, 1)

            dve.wait_ge(ranges, 1)
            dve.wait_ge(ecol_sb, 1)

            def one_hots(b, s):
                if not (isinstance(b, int) and b < 2):
                    dve.wait_ge(c_done, b - 1)
                dve.tensor_scalar(eye[:, s, :], colid[:], rowid[:, bass.ds(b, 1)], None, ALU.is_equal
                                  ).then_inc(eye_done, 1)
                first = dve.value_load(rng_i[0:1, 0, bass.ds(b, 1)], min_val=0, max_val=PAIRS - 1)
                count = dve.value_load(rng_i[0:1, 1, bass.ds(b, 1)], min_val=1, max_val=PAIRS)
                before = dve.value_load(rng_i[0:1, 2, bass.ds(b, 1)], min_val=0, max_val=NB * PAIRS)
                with dve.Fori(0, count) as i:
                    pair = nc.s_assert_within(first + i, 0, PAIRS - 1, skip_runtime_bounds_check_because="a block's pairs end at the last pair")
                    for u in range(2):
                        dve.wait_ge(oh_free, 2 * (before + i) + u + 1)
                        dve.tensor_scalar(oh_dst[:, u, :], colid[:, bass.ds(b * B, B)],
                                          ecol[:, u, bass.ds(pair, 1)], None, ALU.is_equal)
                        dve.tensor_scalar(oh_src[:, u, :], colid[:], ecol[:, 2 + u, bass.ds(pair, 1)], None,
                                          ALU.is_equal).then_inc(oh_done, 1)
            steps(dve, NB, 2, 0, one_hots)

            dve.wait_ge(al_ps, 1)
            dve.tensor_copy(al[:], PS[0:B, 0, 0:2 * H * NB].rearrange("p (b v) -> p v b", v=2 * H)).then_inc(al_sb, 1)
            dve.wait_ge(alr_ps, 1)
            dve.tensor_copy(al_rows[:], PS[0:H * NB, 1, 0:B]).then_inc(alr_sb, 1)

            def maxima(h, b):
                dve_max(dve, NB * h + b, b, arow[:, h, :], nbr, junk, al[:, H + h, bass.ds(b, 1)])

            dve.wait_ge(ld_arow, 16 * H)
            dve.wait_ge(c_done, NB)
            maxima(0, 0)
            maxima(0, 1)
            dve_leaky(dve, 0, 0, prow)
            dve_leaky(dve, 1, 1, prow)
            maxima(0, 2)
            dve_counts(dve, 0, 0, 0, prow)
            dve_counts(dve, 1, 1, 1, prow)
            dve_split(dve, 0, 0, PThi, PTlo)
            dve_leaky(dve, 2, 0, prow)
            for b in range(3, NB):
                maxima(0, b)
            dve_counts(dve, 2, 2, 0, prow)
            dve_split(dve, 1, 1, PThi, PTlo)
            dve_leaky(dve, 3, 1, prow)
            dve.wait_ge(ld_b1, 16)

            for h in range(H):
                def step(j, s):
                    g = NB * h + j
                    more = lambda n: not (h == H - 1 and isinstance(j, int) and j + n >= NB)
                    at = lambda n: j + n - NB if isinstance(j, int) and j + n >= NB else j + n
                    dve.wait_ge(mm_done, 2 * NB * h + NB + j + 1)
                    dve.wait_ge(d_done, g + 1)
                    dve.scalar_tensor_tensor(vbuf[:, s, :], PS[0:B, s, :], rden[:, bass.ds(g, 1)],
                                             b1row[:, h * HC:(h + 1) * HC], ALU.mult, ALU.add).then_inc(v_done, 1)
                    if more(3):
                        dve_counts(dve, g + 3, at(3), 1 - s, prow)
                    last = isinstance(j, int) and j == NB - 1
                    if more(2) and not last:
                        dve_split(dve, g + 2, s, PThi, PTlo)
                    dve.wait_ge(ex_done, g + 1)
                    dve.tensor_scalar(vbuf[:, s, :], vbuf[:, s, :], 0.0, -1.0, ALU.max, ALU.add).then_inc(r_done, 1)
                    dve.wait_ge(r_done, g + 1)
                    dve.scalar_tensor_tensor(ebuf[:, s, :], ebuf[:, s, :], 1.0, vbuf[:, s, :], ALU.min, ALU.add
                                             ).then_inc(hid_done, 1)
                    if more(4) and not last:
                        dve_leaky(dve, g + 4, s, prow)
                    if h + 1 < H and isinstance(j, int) and 6 <= j < 9:
                        maxima(h + 1, j - 6)
                steps(dve, NB, 0, 4, step)
                if h + 1 < H:
                    def make(j, s):
                        split_h(h + 1, j, s)
                        if not (isinstance(j, int) and j >= NB - 3):
                            maxima(h + 1, j + 3)
                    steps(dve, NB, 0, 4, make)
                    dve_split(dve, NB * (h + 1) + 1, 1, PThi, PTlo)
                    dve_leaky(dve, NB * (h + 1) + 3, 1, prow)

            def split_hT(n, half):
                dve.wait_ge(ht_hi, n + 1)
                dve.tensor_tensor(hTlo[:, half, :, :].rearrange("p (a k) n -> p a (k n)", a=2),
                                  PS[:, 4 + 2 * half:6 + 2 * half, 0:4 * B],
                                  hThi[:, half, :, :].bitcast(F32).rearrange("p (a k) n -> p a (k n)", a=2),
                                  ALU.subtract).then_inc(ht_lo, 1)

            split_hT(0, 0)
            for c in range(KC):
                dve.wait_ge(w2_hi, c + 1)
                dve.tensor_tensor(W2lo[:, c, :], w2raw[:, c % 3, :], W2hi[:, c, :].bitcast(F32), ALU.subtract
                                  ).then_inc(w2_lo, 1)
                if c == 2:
                    split_hT(1, 1)
            dve.wait_ge(ld_a2, 32)

            def scores2(b, s):
                dve.wait_ge(h2_sb, b + 1)
                if not (isinstance(b, int) and b == 0):
                    dve.wait_ge(al2_done, 2 * b)
                blk = h2f[:, bass.ds(b, 1), :].rearrange("p o n -> p (o n)")
                for v in range(2):
                    dve.scalar_tensor_tensor(a2junk[:, v, :], blk, 1.0, a2row[:, v, :], ALU.mult, ALU.mult,
                                             accum_out=al2[:, v, bass.ds(b, 1)]).then_inc(al2_done, 1)

            def h2_step(b, s):
                split_hT(2 * b + 2, 0)
                split_hT(2 * b + 3, 1)
                scores2(b, s)
            steps(dve, NB, 2, 2, lambda b, s: h2_step(b, s) if not (isinstance(b, int) and b == NB - 1) else scores2(b, s))
            dve.wait_ge(al2r_ps, 1)
            dve.tensor_copy(al2_rows[:], PS[0:NB, 4, 0:B]).then_inc(al2r_sb, 1)

            G2 = H * NB

            def maxima2(b):
                dve_max(dve, G2 + b, b, arow2[:, 0, :], nbr2, junk2, al2[:, 1, bass.ds(b, 1)])

            def split_h2(b, s):
                dve.wait_ge(h2_hi, b + 1)
                dve.tensor_tensor(h2lo[:, bass.ds(b, 1), :], h2f[:, bass.ds(b, 1), :],
                                  h2hi[:, bass.ds(b, 1), :].bitcast(F32), ALU.subtract).then_inc(h2_lo, 1)
            split_h2(0, 0)
            split_h2(1, 1)
            dve.wait_ge(ld_arow2, 16)
            maxima2(0)
            dve_leaky(dve, G2, 0, prow2)
            maxima2(1)
            dve_leaky(dve, G2 + 1, 1, prow2)
            dve_counts(dve, G2, 0, 0, prow2)
            dve_counts(dve, G2 + 1, 1, 1, prow2)
            dve_split(dve, G2, 0, PT2hi, PT2lo)
            with dve.Fori(1, NB // 2) as k:
                for u in range(2):
                    split_h2(2 * k + u, u)
            maxima2(2)
            dve_leaky(dve, G2 + 2, 0, prow2)
            maxima2(3)
            dve_counts(dve, G2 + 2, 2, 0, prow2)
            dve_split(dve, G2 + 1, 1, PT2hi, PT2lo)
            dve_leaky(dve, G2 + 3, 1, prow2)
            dve.wait_ge(ld_b2, 16)

            def step2(j, s):
                g = G2 + j
                more = lambda n: not (isinstance(j, int) and j + n >= NB)
                yb = y[:, bass.ds(j, 1), :]
                y2 = yb.rearrange("p o (a n) -> p (o a) n", a=2)
                y1 = yb.rearrange("p o n -> p (o n)")
                banks = PS[0:B, 0:2, 0:DH] if s == 0 else PS[0:B, 5:7, 0:DH]
                dve.wait_ge(mm2_done, j + 1)
                dve.wait_ge(d_done, g + 1)
                dve.scalar_tensor_tensor(y2, banks, rden[:, bass.ds(g, 1)],
                                         b2row[:].rearrange("p (a n) -> p a n", a=2), ALU.mult, ALU.add
                                         ).then_inc(y_b, 1)
                if more(3):
                    dve_counts(dve, g + 3, j + 3, 1 - s, prow2)
                if more(2):
                    dve_split(dve, g + 2, s, PT2hi, PT2lo)
                dve.wait_ge(y_b, j + 1)
                dve.wait_ge(ld_xres[s], xres_loaded(j, s))
                dve.tensor_tensor(y1, y1, xres[:, s, :], ALU.add).then_inc(y_x, 1)
                dve.wait_ge(ld_b2, 16)
                dve.wait_ge(y_x, j + 1)
                for a in range(2):
                    last = dve.bn_stats(bnst[:, a, :], y1[:, a * DH:(a + 1) * DH])
                last.then_inc(y_st, 1)
                if more(4):
                    maxima2(j + 4)
                dve.wait_ge(ld_b2, 16)
                dve.wait_ge(y_st, j + 1)
                dve.bn_aggr(mv[:],
                            bnst[:].rearrange("p a n -> p (a n)")).then_inc(y_mv, 1)
                dve.wait_ge(y_mv, j + 1)
                dve.tensor_scalar(vpe[:], mv[:, 1:2], EPS, None, ALU.add
                                  ).then_inc(y_var, 1)
                if more(4):
                    dve_leaky(dve, g + 4, s, prow2)
                dve.wait_ge(y_pow, j + 1)
                dve.tensor_scalar(y1, y1, mv[:, 0:1],
                                  rstd[:, bass.ds(j, 1)], ALU.subtract, ALU.mult).then_inc(y_done, 1)

            def xres_loaded(j, s):
                return 8 * (j - s) + 16
            steps(dve, NB, 0, 4, step2)

        @block.tensor
        def _(pe):
            pe.wait_ge(consts, 8)
            pe.wait_ge(edges_f, 2)
            for n in range(4):
                t = pe.transpose(PS[0:B, 7, n * PAIRS:(n + 1) * PAIRS], (dst_f, src_f)[n // 2][:, n % 2, :],
                                 ident[0:PAIRS, 0:PAIRS])
            t.then_inc(ecol_ps, 1)

            def transpose_x(j, s):
                pe.wait_ge(ld_x[s], 8 * (j - s) + 16)
                if not (isinstance(j, int) and j < 2):
                    pe.wait_ge(xt_lo, j - 1)
                for k in range(KD):
                    t = pe.transpose(PS[:, 2 + 2 * s + k // 4, (k % 4) * B:(k % 4 + 1) * B],
                                     xraw[:, s, k * 128:(k + 1) * 128], ident[0:B, 0:B])
                t.then_inc(xt_ps, 1)
            steps(pe, NB, 2, 0, transpose_x)

            def products(dst, parts, start, stop):
                (ahi, alo), (bhi, blo) = parts
                pe.matmul(dst, ahi, bhi, start=start, stop=False)
                pe.matmul(dst, ahi, blo, start=False, stop=False)
                return pe.matmul(dst, alo, bhi, start=False, stop=stop)

            for j in range(NB):
                if j == 0:
                    pe.wait_ge(xt_lo, NB)
                    pe.wait_ge(w1_lo, KD)
                if j >= 2:
                    pe.wait_ge(h_lo, j - 1)
                for k in range(KD):
                    t = products(PS[0:B, j % 2, :], ((xahi[:, j, k, :], xalo[:, j, k, :]), (W1hi[:, k, :], W1lo[:, k, :])),
                                 k == 0, k == KD - 1)
                t.then_inc(mm_done, 1)

            pe.wait_ge(ranges, 1)
            pe.wait_ge(consts_v, 3)

            def counts(b, s):
                pe.wait_ge(eye_done, b + 1)
                if not (isinstance(b, int) and b < 2):
                    pe.wait_ge(c_done, b - 1)
                for c, (lo, hi) in enumerate(CCH):
                    t = pe.matmul(count_bank(s, c), ident_b[0:B, 0:B], eye[:, s, lo:hi], start=True, stop=False,
                                  skip_group_check=True)
                if isinstance(b, int) and b == 0:
                    t.then_inc(oh_free, 2)
                count = pe.value_load(rng_i[0:1, 1, bass.ds(b, 1)], min_val=1, max_val=PAIRS)
                before = pe.value_load(rng_i[0:1, 2, bass.ds(b, 1)], min_val=0, max_val=NB * PAIRS)
                with pe.Fori(0, count) as i:
                    for u in range(2):
                        pe.wait_ge(oh_done, 2 * (before + i) + u + 1)
                        for c, (lo, hi) in enumerate(CCH):
                            t = pe.matmul(count_bank(s, c), oh_dst[:, u, :], oh_src[:, u, lo:hi], start=False,
                                          stop=False, skip_group_check=True)
                        t.then_inc(oh_free, 1)
            steps(pe, NB, 2, 0, counts)

            pe.wait_ge(h_lo, NB)
            pe.wait_ge(wa_hi, 1)
            pe.wait_ge(wa_lo, 1)
            for j in range(NB):
                for k in range(KD):
                    t = products(PS[0:B, 0, 2 * H * j:2 * H * (j + 1)],
                                 ((xahi[:, j, k, :], xalo[:, j, k, :]), (wahi[:, k, :], walo[:, k, :])),
                                 k == 0, k == KD - 1)
            t.then_inc(al_ps, 1)
            pe.wait_ge(al_sb, 1)
            pe.transpose(PS[0:H * NB, 1, 0:B], al[:, 0:H, :].rearrange("p v b -> p (v b)"), ident[0:B, 0:B]
                         ).then_inc(alr_ps, 1)

            pe.wait_ge(c_done, NB)
            pe.wait_ge(alr_sb, 1)
            pe.wait_ge(pc_done, 1)
            pe_transpose(pe, 0, 0, prow)

            for h in range(H):
                def step(j, s):
                    g = NB * h + j
                    if not (h == H - 1 and isinstance(j, int) and j == NB - 1):
                        pe.wait_ge(pc_done, g + 2)
                        pe.wait_ge(pt_lo, g + 1)
                        pe_transpose(pe, g + 1, 1 - s, prow)
                    else:
                        pe.wait_ge(pt_lo, g + 1)
                    if isinstance(j, int) and j < 2:
                        pe.wait_ge(h_lo, NB * (h + 1))
                    else:
                        pe.wait_ge(v_done, g - 1)
                    for b in range(NB):
                        t = products(PS[0:B, s, :], ((PThi[:, s, b, :], PTlo[:, s, b, :]), (hhi[:, b, :], hlo[:, b, :])),
                                     b == 0, b == NB - 1)
                    t.then_inc(mm_done, 1)
                steps(pe, NB, 2, 2, step)
                if h + 1 < H:
                    def make(j, s):
                        if isinstance(j, int) and j < 2:
                            pe.wait_ge(w1_hi, KD * (h + 2))
                            pe.wait_ge(w1_lo, KD * (h + 2))
                            pe.wait_ge(v_done, NB * (h + 1) - 1 + j)
                        else:
                            pe.wait_ge(h_lo, NB * (h + 1) + j - 1)
                        pe.wait_ge(ld_xr[s], 16 * (NB // 2) * h + 8 * (j - s) + 16)
                        for k in range(KD):
                            t = products(PS[0:B, s, :],
                                         ((xr[:, s, 0, k * B:(k + 1) * B], xr[:, s, 1, k * B:(k + 1) * B]),
                                          (W1hi[:, k, :], W1lo[:, k, :])), k == 0, k == KD - 1)
                        t.then_inc(mm_done, 1)
                    steps(pe, NB, 2, 0, make)

            pe.wait_ge(v_done, H * NB)

            def transpose_h(b, s, half):
                if half == 0:
                    pe.wait_ge(ld_hb[s], 8 * (b - s) + 16)
                if not (isinstance(b, int) and b == 0):
                    pe.wait_ge(ht_lo, 2 * b + half - 1)
                for k in range(KH):
                    t = pe.transpose(PS[:, 4 + 2 * half + k // 4, (k % 4) * B:(k % 4 + 1) * B],
                                     hblk[:, s, (half * KH + k) * 128:(half * KH + k + 1) * 128], ident[0:B, 0:B])
                t.then_inc(ht_ps, 1)

            def mm_half(b, s, half):
                pe.wait_ge(ht_lo, 2 * b + half + 1)
                for k in range(KH):
                    c = half * KH + k
                    if isinstance(b, int) and b == 0:
                        pe.wait_ge(w2_lo, c + 1)
                    for a in range(2):
                        t = products(PS[0:B, 2 * s + a, 0:DH],
                                     ((hThi[:, half, k, :], hTlo[:, half, k, :]),
                                      (W2hi[:, c, a * DH:(a + 1) * DH], W2lo[:, c, a * DH:(a + 1) * DH])),
                                     c == 0, c == KC - 1)
                t.then_inc(h2_ps, 1)

            transpose_h(0, 0, 0)
            transpose_h(0, 0, 1)

            def h2_block(b, s):
                if not (isinstance(b, int) and b < 2):
                    pe.wait_ge(h2_sb, b - 1)
                mm_half(b, s, 0)
                if not (isinstance(b, int) and b == NB - 1):
                    transpose_h(b + 1, 1 - s, 0)
                mm_half(b, s, 1)
                if not (isinstance(b, int) and b == NB - 1):
                    transpose_h(b + 1, 1 - s, 1)
            steps(pe, NB, 2, 2, h2_block)
            pe.wait_ge(al2_done, 2 * NB)
            pe.transpose(PS[0:NB, 4, 0:B], al2[:, 0, :], ident[0:B, 0:B]).then_inc(al2r_ps, 1)

            G2 = H * NB
            pe.wait_ge(al2r_sb, 1)
            pe.wait_ge(h2_sb, NB)
            pe.wait_ge(pc_done, G2 + 1)
            pe_transpose(pe, G2, 0, prow2)

            def step2(j, s):
                g = G2 + j
                if not (isinstance(j, int) and j == NB - 1):
                    pe.wait_ge(pc_done, g + 2)
                    pe.wait_ge(pt_lo, g + 1)
                    pe_transpose(pe, g + 1, 1 - s, prow2)
                else:
                    pe.wait_ge(pt_lo, g + 1)
                if not (isinstance(j, int) and j < 2):
                    pe.wait_ge(y_b, j - 1)
                for b in range(NB):
                    if isinstance(j, int) and j == 0:
                        pe.wait_ge(h2_lo, b + 1)
                    for a in range(2):
                        t = products(PS[0:B, 5 * s + a, 0:DH],
                                     ((PT2hi[:, s, b, :], PT2lo[:, s, b, :]),
                                      (h2hi[:, b, a * DH:(a + 1) * DH], h2lo[:, b, a * DH:(a + 1) * DH])),
                                     b == 0, b == NB - 1)
                t.then_inc(mm2_done, 1)
            steps(pe, NB, 2, 2, step2)


_INS = ["x", "src", "dst", "L0_gnn_W1", "L0_gnn_att_src1", "L0_gnn_att_dst1", "L0_gnn_b1",
        "L0_gnn_W2", "L0_gnn_att_src2", "L0_gnn_att_dst2", "L0_gnn_b2"]


def kernel(**inputs):
    import numpy as _np
    import concourse.bacc as _bacc
    from concourse import mybir as _mybir
    from concourse.bass_utils import run_bass_kernel_spmd as _run

    nc = _bacc.Bacc("TRN2", target_bir_lowering=False, num_devices=1)
    arrays, args = {}, []
    for name in _INS:
        a = _np.ascontiguousarray(inputs[name])
        arrays[f"in_{name}"] = a
        args.append(nc.dram_tensor(f"in_{name}", a.shape, _mybir.dt.from_np(a.dtype), kind="ExternalInput").ap())
    args.append(nc.dram_tensor("out_0", (N, D), F32, kind="ExternalOutput").ap())
    gat_kernel(nc, *args)
    r = _run(nc, [arrays], core_ids=[0])
    return r.results[0]["out_0"]
```

```python
from contextlib import ExitStack

import concourse.bass as bass
from concourse import mybir

F32 = mybir.dt.float32
F32R = mybir.dt.float32r
BF16 = mybir.dt.bfloat16
U16 = mybir.dt.uint16
I32 = mybir.dt.int32
ALU = mybir.AluOpType
ACT = mybir.ActivationFunctionType
AX = mybir.AxisListType
RMAX = bass.bass_isa.ReduceOp.max

N = 1250
E = 20000
B = 125
NB = N // B
PAIRS = E // (2 * B)
D = 768
H = 4
HC = 512
KD = D // 128
HID = H * HC
KC = HID // 128
KH = KC // 2
DH = D // 2
SLOPE = 0.2
EPS = 1e-5
MASKED = -1.0e30
BANK = 512
BB = 4
CW = BB * B
TCH = [(0, BB), (BB, 2 * BB), (2 * BB, NB)]
SLOTS = 4
DSLOTS = 2 * SLOTS
QUADS = PAIRS // 2
XL = 2


def steps(eng, n, front, back, body, m=2):
    for j in range(front):
        body(j, j % m)
    if n - back > front:
        with eng.Fori(front // m, (n - back) // m) as k:
            for u in range(m):
                body(m * k + u, u)
    for j in range(n - back, n):
        body(j, j % m)


PROLOGUE = ([("counts", 0), ("x", 0), ("counts", 1), ("h", 0), ("fold", 0), ("counts", 2), ("h", 1), ("fold", 1), ("fold", 2)]
            + [("counts", 3), ("h", 2), ("fold", 3), ("fold", 4), ("counts", 4), ("h", 3), ("fold", 5), ("fold", 6)]
            + [("counts", 5), ("h", 4), ("fold", 7), ("fold", 8), ("counts", 6), ("h", 5), ("fold", 9)]
            + [("counts", 7), ("h", 6), ("fold", 10), ("counts", 8), ("h", 7), ("fold", 11)]
            + [("scores", 0), ("scores", 1), ("counts", 9)])


def gat_kernel(nc, x, src, dst, W1, as1, ad1, b1, W2, as2, ad2, b2, out):
    xT_d = nc.dram_tensor("xT_scratch", (NB, 128, 2, KD * B), F32, kind="Internal").ap()
    hid_d = nc.dram_tensor("hidden_scratch", (N, HID), F32, kind="Internal").ap()

    with ExitStack() as ctx:
        def sem(name):
            return ctx.enter_context(nc.semaphore(name))

        cursor = [((nc.sbuf_base + 31) // 32) * 32]
        top = [cursor[0]]

        def sb(name, shape, dt):
            size = 1
            for s in shape[1:]:
                size *= s
            size *= {F32: 4, F32R: 4, I32: 4, BF16: 2, U16: 2}[dt]
            t = nc.alloc_sbuf_tensor_at(name, shape, dt, offset=cursor[0])
            cursor[0] += ((size + 31) // 32) * 32
            top[0] = max(top[0], cursor[0])
            return t

        C = sb("counts", [B, NB, N], U16)
        ident = sb("ident", [128, 128], F32)
        ident_b = sb("ident_b", [128, 128], BF16)
        colid = sb("colid", [B, N], U16)
        al = sb("al", [B, 2 * H, NB], F32)
        zero = sb("zero", [B, 1], F32)
        one = sb("one", [B, 1], F32)
        negm = sb("negm", [B, (H + 1) * NB], F32)
        rden = sb("rden", [B, (H + 1) * NB], F32)
        mx = sb("mx", [B, 1], F32)
        gate = sb("gate", [B, 1], F32)
        mneg = sb("mneg", [B, 1], F32)
        den = sb("den", [B, 1], F32)
        deps = sb("deps", [B, 1], F32)
        al2 = sb("al2", [B, 2, NB], F32)
        bnst = sb("bnst", [B, 2, 6], F32)
        mv = sb("mv", [B, 2], F32)
        vpe = sb("vpe", [B, 1], F32)
        rstd = sb("rstd", [B, NB], F32)
        mhalf = sb("mhalf", [B, 1], F32)
        base0 = cursor[0]

        W1hi = sb("W1hi", [128, KD, HC], F32R)
        W1lo = sb("W1lo", [128, KD, HC], F32R)
        w1raw = sb("w1raw", [128, KD, HC], F32)
        hhi = sb("hhi", [B, NB, HC], F32R)
        hlo = sb("hlo", [B, NB, HC], F32R)
        base1 = cursor[0]
        cursor[0] = base1 - 2 * NB * HC * 4
        xall = sb("xall", [B, NB, D], F32)

        cursor[0] = base1
        xahi = sb("xahi", [128, KD, NB, B], F32R)
        xalo = sb("xalo", [128, KD, NB, B], F32R)
        attr = sb("attr", [128, 2 * H, HC], F32)
        wa_f = sb("wa_f", [128, KD, 2 * H], F32)
        wahi = sb("wahi", [128, KD, 2 * H], F32R)
        walo = sb("walo", [128, KD, 2 * H], F32R)
        junk_w = sb("junk_w", [128, 2, HC], BF16)
        dst_i = sb("dst_i", [PAIRS, 2, B], I32)
        src_i = sb("src_i", [PAIRS, 2, B], I32)
        dst_f = sb("dst_f", [PAIRS, 2, B], F32)
        src_f = sb("src_f", [PAIRS, 2, B], F32)
        blk_lo = sb("blk_lo", [PAIRS, NB], F32)
        blk_hi = sb("blk_hi", [PAIRS, NB], F32)
        pairid = sb("pairid", [PAIRS, 1], F32)
        pairrv = sb("pairrv", [PAIRS, 1], F32)
        dmin = sb("dmin", [PAIRS, 1], F32)
        dmax = sb("dmax", [PAIRS, 1], F32)
        hit = sb("hit", [PAIRS, 3, NB], F32)
        key = sb("key", [PAIRS, 2 * NB], F32)
        keyr = sb("keyr", [PAIRS, 2 * NB], F32)
        rng_f = sb("rng_f", [1, 5, NB], F32)
        ones1 = sb("ones1", [1, NB], F32)
        live_late = cursor[0]
        rows = sb("rows", [2 * H, N], F32)
        oh_src = sb("oh_src", [B, SLOTS, N], BF16)
        oh_dst = sb("oh_dst", [B, 2, SLOTS, B], BF16)
        oh_sq = sb("oh_sq", [B, 2, 2, 2, B], BF16)
        ecol = sb("ecol", [B, 4, PAIRS], F32)
        rng_i = sb("rng_i", [1, 5, NB], I32)

        cursor[0] = base1
        PThi = sb("PThi", [B, 2, NB, B], F32R)
        PTlo = sb("PTlo", [B, 2, NB, B], F32R)
        xr = sb("xr", [128, 2, 2, KD * B], F32R)
        b1row = sb("b1row", [B, HID], F32)
        vbuf = sb("vbuf", [B, 2, HC], F32)
        ebuf = sb("ebuf", [B, 2, HC], F32)
        arow = sb("arow", [B, H, N], F32)
        assert cursor[0] - N * 4 >= base1 + 2 * NB * KD * B * 4
        prow = sb("prow", [B, 2, N], F32)
        nbr = sb("nbr", [B, N], BF16)
        junk = sb("junk", [B, N], BF16)
        assert cursor[0] <= live_late

        cursor[0] = base0
        W2hi = sb("W2hi", [128, KC, D], F32R)
        W2lo = sb("W2lo", [128, KC, D], F32R)
        h2f = sb("h2f", [B, NB, D], F32)
        hThi = sb("hThi", [128, 2, KH, B], F32R)
        hTlo = sb("hTlo", [128, 2, KH, B], F32R)
        hblk = sb("hblk", [B, 2, HID], F32)
        a2row = sb("a2row", [B, 2, D], F32)
        w2raw = sb("w2raw", [128, 3, D], F32)
        a2junk = sb("a2junk", [B, 2, D], BF16)

        cursor[0] = base0
        h2hi = sb("h2hi", [B, NB, D], F32R)
        h2lo = sb("h2lo", [B, NB, D], F32R)
        prow2 = sb("prow2", [B, 2, N], F32)
        PT2hi = sb("PT2hi", [B, 2, NB, B], F32R)
        PT2lo = sb("PT2lo", [B, 2, NB, B], F32R)
        arow2 = sb("arow2", [B, N], F32)
        assert cursor[0] <= base0 + 2 * KC * D * 4
        cursor[0] = base0 + 2 * KC * D * 4 + NB * D * 4
        y = sb("y", [B, NB, D], F32)
        b2row = sb("b2row", [B, D], F32)
        xres = sb("xres", [B, 2, D], F32)
        nbr2 = sb("nbr2", [B, N], BF16)
        junk2 = sb("junk2", [B, N], BF16)
        assert top[0] <= nc.sbuf_usable_end, (top[0], nc.sbuf_usable_end)

        PS = ctx.enter_context(nc.psum_tensor("ps", [128, 8, BANK], F32))

        ld_edges = sem("ld_edges")
        ld_x = [sem(f"ld_x{i}") for i in range(NB // XL)]
        ld_w1 = sem("ld_w1")
        ld_att = sem("ld_att")
        ld_wk = [sem(f"ld_wk{i}") for i in range(3)]
        xT_stored = sem("xT_stored")
        ld_b1 = sem("ld_b1")
        ld_xr = [sem(f"ld_xr{i}") for i in range(2)]
        hid_stored = [sem(f"hid_stored{i}") for i in range(2)]
        ld_hb = [sem(f"ld_hb{i}") for i in range(2)]
        ld_a2 = sem("ld_a2")
        ld_w2 = [sem(f"ld_w2{i}") for i in range(3)]
        ld_b2 = sem("ld_b2")
        ld_xres = [sem(f"ld_xres{i}") for i in range(2)]
        out_stored = sem("out_stored")

        consts = sem("consts")
        consts_v = sem("consts_v")
        edges_f = sem("edges_f")
        ecol_ps = sem("ecol_ps")
        ecol_sb = sem("ecol_sb")
        plan = sem("plan")
        keys_red = sem("keys_red")
        ranges = sem("ranges")
        xt_ps = sem("xt_ps")
        xt_hi = sem("xt_hi")
        xt_lo = sem("xt_lo")
        w1_hi = sem("w1_hi")
        w1_lo = sem("w1_lo")
        h_hi = sem("h_hi")
        h_lo = sem("h_lo")
        mm_done = sem("mm_done")
        wa_done = sem("wa_done")
        wa_hi = sem("wa_hi")
        wa_lo = sem("wa_lo")
        zeroed = sem("zeroed")
        oh_done = sem("oh_done")
        sq_done = sem("sq_done")
        ohd_done = sem("ohd_done")
        oh_free = sem("oh_free")
        c_done = sem("c_done")
        rows_ps = sem("rows_ps")
        rows_sb = sem("rows_sb")
        al_ps = sem("al_ps")
        al_sb = sem("al_sb")
        bc_ps = sem("bc_ps")
        bc_sb = sem("bc_sb")
        m_nb = sem("m_nb")
        m_max = sem("m_max")
        m_neg = sem("m_neg")
        m_done = sem("m_done")
        z_done = sem("z_done")
        e_done = sem("e_done")
        p_done = sem("p_done")
        pc_done = sem("pc_done")
        d_eps = sem("d_eps")
        d_done = sem("d_done")
        t_done = sem("t_done")
        pt_hi = sem("pt_hi")
        pt_lo = sem("pt_lo")
        v_done = sem("v_done")
        ex_done = sem("ex_done")
        r_done = sem("r_done")
        hid_done = sem("hid_done")
        w2_hi = sem("w2_hi")
        w2_lo = sem("w2_lo")
        ht_ps = sem("ht_ps")
        ht_hi = sem("ht_hi")
        ht_lo = sem("ht_lo")
        h2_ps = sem("h2_ps")
        h2_sb = sem("h2_sb")
        al2_done = sem("al2_done")
        bc2_ps = sem("bc2_ps")
        bc2_sb = sem("bc2_sb")
        h2_hi = sem("h2_hi")
        h2_lo = sem("h2_lo")
        mm2_done = sem("mm2_done")
        y_b = sem("y_b")
        y_x = sem("y_x")
        y_st = sem("y_st")
        y_mv = sem("y_mv")
        y_var = sem("y_var")
        y_pow = sem("y_pow")
        y_done = sem("y_done")

        def count_bank(s, c):
            return PS[0:B, 2 + 3 * s + c, 0:(TCH[c][1] - TCH[c][0]) * B]

        def x_banks(s):
            return (0, 5, 2)[s]

        block = ctx.enter_context(nc.Block())

        def edge_steps(eng, b):
            return (eng.value_load(rng_i[0:1, 0, b:b + 1], min_val=0, max_val=PAIRS - 2),
                    eng.value_load(rng_i[0:1, 1, b:b + 1], min_val=1, max_val=QUADS),
                    eng.value_load(rng_i[0:1, 2, b:b + 1], min_val=0, max_val=NB * QUADS))

        def at_pair(first, i, v):
            return nc.s_assert_within(first + 2 * i + v, 0, PAIRS - 1,
                                      skip_runtime_bounds_check_because="a block's steps end at the last pair")

        @block.sync
        def _(sp):
            sp.dma_start(dst_i[:], dst.rearrange("(p u e) -> p u e", u=2, e=B)).then_inc(ld_edges, 16)
            sp.dma_start(src_i[:], src.rearrange("(p u e) -> p u e", u=2, e=B)).then_inc(ld_edges, 16)

            for i in range(NB // XL):
                sp.dma_start(xall[:, XL * i:XL * (i + 1), :], x[XL * i * B:XL * (i + 1) * B, :]
                             .rearrange("(b p) d -> p b d", p=B)).then_inc(ld_x[i], 16)

            def load_w1(h):
                sp.dma_start(w1raw[:], W1[:, h * HC:(h + 1) * HC].rearrange("(k p) c -> p k c", p=128)
                             ).then_inc(ld_w1, 16)

            load_w1(0)
            sp.dma_start(attr[:, 0:H, :], as1.rearrange("(o h) c -> o h c", o=1).broadcast_to([128, H, HC])
                         ).then_inc(ld_att, 16)
            sp.dma_start(attr[:, H:2 * H, :], ad1.rearrange("(o h) c -> o h c", o=1).broadcast_to([128, H, HC])
                         ).then_inc(ld_att, 16)

            def store_xT(j, s):
                sp.wait_ge(xt_hi, j + 1)
                sp.wait_ge(xt_lo, j + 1)
                sp.dma_start(xT_d[bass.ds(j, 1), :, 0, :].rearrange("o p (k n) -> (o p) k n", k=KD),
                             xahi[:, :, bass.ds(j, 1), :].bitcast(F32).rearrange("p k o n -> p k (o n)")).then_inc(xT_stored, 16)
                sp.dma_start(xT_d[bass.ds(j, 1), :, 1, :].rearrange("o p (k n) -> (o p) k n", k=KD),
                             xalo[:, :, bass.ds(j, 1), :].bitcast(F32).rearrange("p k o n -> p k (o n)")).then_inc(xT_stored, 16)
            steps(sp, NB, 0, 0, store_xT)

            sp.wait_ge(w1_hi, KD)
            sp.wait_ge(w1_lo, KD)
            for n in range(2 * KD):
                if n >= 3:
                    sp.wait_ge(wa_done, H * (n - 2))
                sp.dma_start(w1raw[:, 2 * (n % 3):2 * (n % 3) + 2, :],
                             W1[128 * (n // 2):128 * (n // 2) + 128, bass.ts(n % 2, 2 * HC)]
                             .rearrange("p (a c) -> p a c", a=2)).then_inc(ld_wk[n % 3], 16)
            sp.wait_ge(wa_done, 2 * H * KD)
            load_w1(1)

            sp.wait_ge(rows_ps, 3)
            sp.wait_ge(mm_done, NB)
            sp.wait_ge(xT_stored, 32 * NB)
            sp.dma_start(b1row[:], b1.rearrange("(o n) -> o n", o=1).broadcast_to([B, HID])).then_inc(ld_b1, 16)

            def load_xr(h, j, s):
                if not (h == 1 and isinstance(j, int) and j < 2):
                    sp.wait_ge(mm_done, slot_free(h, j))
                sp.dma_start(xr[:, s, :, :].bitcast(F32), xT_d[bass.ds(j, 1), :, :, :].rearrange("o p t n -> p (o t) n")
                             ).then_inc(ld_xr[s], 16)

            def slot_free(h, j):
                if isinstance(j, int) and j < 2:
                    return 20 * (h - 1) + NB - 2 + j + 1
                return 20 * h + j - 1

            def store_hid(h, j, s):
                sp.wait_ge(hid_done, NB * h + j + 1)
                sp.dma_start(hid_d[bass.ds(j * B, B), h * HC:(h + 1) * HC], ebuf[:, s, :]).then_inc(hid_stored[s], 16)

            for h in range(H):
                if h + 1 < H:
                    load_xr(h + 1, 0, 0)
                    load_xr(h + 1, 1, 1)
                steps(sp, NB, 0, 0, lambda j, s: store_hid(h, j, s))
                if h + 2 < H:
                    sp.wait_ge(w1_hi, KD * (h + 2))
                    sp.wait_ge(w1_lo, KD * (h + 2))
                    load_w1(h + 2)
                if h + 1 < H:
                    with sp.Fori(1, NB // 2) as k:
                        for u in range(2):
                            load_xr(h + 1, 2 * k + u, u)

            sp.wait_ge(mm_done, 2 * H * NB)
            sp.wait_ge(v_done, H * NB)
            for i in range(2):
                sp.wait_ge(hid_stored[i], 16 * H * NB // 2)

            def load_w2(c):
                if c >= 3:
                    sp.wait_ge(w2_hi, c - 2)
                    sp.wait_ge(w2_lo, c - 2)
                sp.dma_start(w2raw[:, c % 3, :], W2[128 * c:128 * c + 128, :]).then_inc(ld_w2[c % 3], 16)

            def load_hb(b, s):
                if not (isinstance(b, int) and b < 2):
                    sp.wait_ge(ht_ps, 2 * b - 2)
                sp.dma_start(hblk[:, s, :], hid_d[bass.ds(b * B, B), :]).then_inc(ld_hb[s], 16)

            load_hb(0, 0)
            for c in range(3):
                load_w2(c)
            load_hb(1, 1)
            sp.dma_start(a2row[:, 0, :], as2.broadcast_to([B, D])).then_inc(ld_a2, 16)
            sp.dma_start(a2row[:, 1, :], ad2.broadcast_to([B, D])).then_inc(ld_a2, 16)
            for c in range(3, KC):
                load_w2(c)
            with sp.Fori(1, NB // 2) as k:
                for u in range(2):
                    load_hb(2 * k + u, u)

            sp.wait_ge(al2_done, 2 * NB)
            sp.dma_start(b2row[:], b2.rearrange("(o n) -> o n", o=1).broadcast_to([B, D])).then_inc(ld_b2, 16)

            def load_xres(b, s):
                if not (isinstance(b, int) and b < 2):
                    sp.wait_ge(y_x, b - 1)
                sp.dma_start(xres[:, s, :], x[bass.ds(b * B, B), :]).then_inc(ld_xres[s], 16)

            def store_out(b, s):
                sp.wait_ge(y_done, b + 1)
                sp.dma_start(out[bass.ds(b * B, B), :], y[:, bass.ds(b, 1), :].rearrange("p o n -> p (o n)")
                             ).then_inc(out_stored, 16)

            load_xres(0, 0)
            load_xres(1, 1)
            with sp.Fori(1, NB // 2) as k:
                for u in range(2):
                    load_xres(2 * k + u, u)
                    store_out(2 * k + u - 2, u)
            store_out(NB - 2, 0)
            store_out(NB - 1, 1)
            sp.wait_ge(out_stored, 16 * NB)

        @block.gpsimd
        def _(pool):
            pool.memset(ident[:], 0.0).then_inc(consts, 1)
            pool.iota(colid[:], [[1, N]], base=0, channel_multiplier=0).then_inc(consts, 1)
            pool.memset(zero[:], 0.0)
            pool.memset(one[:], 1.0).then_inc(consts, 1)
            pool.iota(blk_lo[:], [[B, NB]], base=0, channel_multiplier=0,
                      allow_small_or_imprecise_dtypes=True).then_inc(consts, 1)
            pool.iota(blk_hi[:], [[B, NB]], base=B, channel_multiplier=0,
                      allow_small_or_imprecise_dtypes=True).then_inc(consts, 1)
            pool.iota(pairid[:], [[1, 1]], base=1, channel_multiplier=1,
                      allow_small_or_imprecise_dtypes=True).then_inc(consts, 1)
            pool.iota(pairrv[:], [[1, 1]], base=PAIRS, channel_multiplier=-1,
                      allow_small_or_imprecise_dtypes=True).then_inc(consts, 1)
            pool.wait_ge(consts, 7)
            pool.affine_select(out=ident[:], in_=ident[:], compare_op=ALU.not_equal, fill=1.0, base=0,
                               pattern=[[-1, 128]], channel_multiplier=1).then_inc(consts, 1)
            pool.wait_ge(plan, 6)
            pool.partition_all_reduce(keyr[:], key[:], PAIRS, RMAX).then_inc(keys_red, 1)

            def split_w1(h, k):
                pool.wait_ge(w1_hi, KD * h + k + 1)
                pool.tensor_tensor(W1lo[:, bass.ds(k, 1), :], w1raw[:, bass.ds(k, 1), :],
                                   W1hi[:, bass.ds(k, 1), :].bitcast(F32), ALU.subtract).then_inc(w1_lo, 1)

            for k in range(KD):
                split_w1(0, k)

            for h in range(1, H):
                steps(pool, KD, 0, 0, lambda k, s: split_w1(h, k))

            def pow_var(b, s):
                pool.wait_ge(y_var, b + 1)
                pool.tensor_tensor(rstd[:, bass.ds(b, 1)], vpe[:], mhalf[:], ALU.pow).then_inc(y_pow, 1)
            steps(pool, NB, 0, 0, pow_var)

        def act_scores(act, s, buf, row, dcol):
            act.activation(buf[:, s, :], row, ACT.Identity, bias=dcol).then_inc(z_done, 1)

        def act_exp(act, g, s, buf):
            act.wait_ge(e_done, g + 1)
            act.wait_ge(m_done, g + 1)
            act.activation(buf[:, s, :], buf[:, s, :], ACT.Exp, bias=negm[:, bass.ds(g, 1)]).then_inc(p_done, 1)

        def act_split(act, g, s, hi):
            act.wait_ge(t_done, g + 1)
            act.activation(hi[:, s, 0:8, :].rearrange("p (a b) n -> p a (b n)", a=2),
                           PS[0:B, 2:4, 0:4 * B], ACT.Copy)
            act.activation(hi[:, s, 8:10, :].rearrange("p b n -> p (b n)"),
                           PS[0:B, 4, 0:2 * B], ACT.Copy).then_inc(pt_hi, 1)

        def dve_max(dve, g, b, row, scr, jnk, dcol):
            dve.tensor_scalar(scr[:], C[:, bass.ds(b, 1), :].rearrange("p o n -> p (o n)"), 0.0, MASKED,
                              ALU.is_equal, ALU.mult).then_inc(m_nb, 1)
            dve.wait_ge(m_nb, g + 1)
            dve.memset(gate[:], 0.0)
            dve.tensor_tensor_reduce(out=jnk[:], in0=scr[:], in1=row, scale=1.0, scalar=-3.0e38,
                                     op0=ALU.add, op1=ALU.max, accum_out=mx[:]).then_inc(m_max, 1)
            dve.wait_ge(m_max, g + 1)
            dve.scalar_tensor_tensor(mneg[:], mx[:], -1.0, dcol, ALU.mult, ALU.subtract).then_inc(m_neg, 1)
            dve.wait_ge(m_neg, g + 1)
            dve.scalar_tensor_tensor(negm[:, bass.ds(g, 1)], mneg[:], SLOPE, mneg[:], ALU.mult, ALU.min
                                     ).then_inc(m_done, 1)

        def dve_leaky(dve, g, s, buf):
            dve.wait_ge(z_done, g + 1)
            dve.scalar_tensor_tensor(buf[:, s, :], buf[:, s, :], SLOPE, buf[:, s, :], ALU.mult, ALU.max
                                     ).then_inc(e_done, 1)

        def dve_counts(dve, g, b, s, buf):
            dve.wait_ge(p_done, g + 1)
            dve.scalar_tensor_tensor(buf[:, s, :], buf[:, s, :], 1.0,
                                     C[:, bass.ds(b, 1), :].rearrange("p o n -> p (o n)"),
                                     ALU.min, ALU.mult, accum_out=den[:]).then_inc(pc_done, 1)
            dve.wait_ge(pc_done, g + 1)
            dve.tensor_scalar(deps[:], den[:], 1e-16, None, ALU.add).then_inc(d_eps, 1)
            dve.wait_ge(d_eps, g + 1)
            dve.reciprocal(rden[:, bass.ds(g, 1)], deps[:]).then_inc(d_done, 1)

        def dve_split(dve, g, s, hi, lo):
            dve.wait_ge(pt_hi, g + 1)
            dve.tensor_tensor(lo[:, s, 0:8, :].rearrange("p (a b) n -> p a (b n)", a=2), PS[0:B, 2:4, 0:4 * B],
                              hi[:, s, 0:8, :].bitcast(F32).rearrange("p (a b) n -> p a (b n)", a=2), ALU.subtract)
            dve.tensor_tensor(lo[:, s, 8:10, :].rearrange("p b n -> p (b n)"), PS[0:B, 4, 0:2 * B],
                              hi[:, s, 8:10, :].bitcast(F32).rearrange("p b n -> p (b n)"), ALU.subtract
                              ).then_inc(pt_lo, 1)

        def pe_transpose(pe, g, s, buf):
            for bank, (lo, hi) in enumerate(TCH):
                for b in range(lo, hi):
                    t = pe.transpose(PS[0:B, 2 + bank, (b - lo) * B:(b - lo + 1) * B],
                                     buf[:, s, b * B:(b + 1) * B], ident[0:B, 0:B])
            t.then_inc(t_done, 1)

        @block.scalar
        def _(act):
            def split_xT(j, s):
                act.wait_ge(xt_ps, j + 1)
                p = x_banks(s)
                act.activation(xahi[:, 0:4, bass.ds(j, 1), :].rearrange("p k o n -> p k (o n)"),
                               PS[:, p, 0:4 * B].rearrange("p (k n) -> p k n", k=4), ACT.Copy)
                act.activation(xahi[:, 4:6, bass.ds(j, 1), :].rearrange("p k o n -> p k (o n)"),
                               PS[:, p + 1, 0:2 * B].rearrange("p (k n) -> p k n", k=2), ACT.Copy).then_inc(xt_hi, 1)

            def split_w1(k):
                act.activation(W1hi[:, bass.ds(k, 1), :], w1raw[:, bass.ds(k, 1), :], ACT.Copy).then_inc(w1_hi, 1)

            def split_h(h, j, s):
                act.wait_ge(mm_done, 2 * NB * h + j + 1)
                act.activation(hhi[:, bass.ds(j, 1), :].rearrange("p o c -> p (o c)"), PS[0:B, s, :], ACT.Copy
                               ).then_inc(h_hi, 1)

            def clear(b):
                if b >= 2:
                    act.wait_ge(c_done, b - 1)
                act.activation(PS[0:B, 2 + 3 * (b % 2):5 + 3 * (b % 2), 0:CW],
                               zero[:].rearrange("p (o n) -> p o n", o=1).broadcast_to([B, 3, CW]), ACT.Copy
                               ).then_inc(zeroed, 1)

            def one_hots(b):
                first, count, before = edge_steps(act, b)
                with act.Fori(0, count) as i:
                    turn = (before + i) % 2
                    for v in range(2):
                        pair = at_pair(first, i, v)
                        half = 2 * (before + i) + v
                        sq_v = oh_sq[:, bass.ds(turn, 1), v, :, :].rearrange("p o u n -> p (o u n)")
                        act.wait_ge(oh_free, 2 * half + 2)
                        for u in range(2):
                            sq = act.activation(sq_v[:, u * B:(u + 1) * B], colid[:, b * B:(b + 1) * B], ACT.Square, scale=-1.0,
                                                bias=ecol[:, u, bass.ds(pair, 1)])
                        sq.then_inc(sq_done, 1)
                        act.wait_ge(sq_done, half + 1)
                        act.activation(oh_dst[:, bass.ds(turn, 1), 2 * v:2 * v + 2, :].rearrange("p o u n -> p (o u n)"),
                                       sq_v, ACT.Relu, scale=-1.0, bias=one[:]).then_inc(ohd_done, 1)

            def counts_out(b):
                last = act.value_load(rng_i[0:1, 4, b:b + 1], min_val=SLOTS + DSLOTS, max_val=SLOTS * NB * QUADS + DSLOTS)
                act.wait_ge(oh_free, last)
                s = b % 2
                act.activation(C[:, b, 0:2 * CW].rearrange("p (a n) -> p a n", a=2),
                               PS[0:B, 2 + 3 * s:4 + 3 * s, 0:CW], ACT.Copy)
                act.activation(C[:, b, 2 * CW:N], count_bank(s, 2), ACT.Copy).then_inc(c_done, 1)

            def row_out(to, set_):
                p = 2 + 3 * set_
                act.activation(to[:, 0:2 * CW].rearrange("p (a n) -> p a n", a=2), PS[0:B, p:p + 2, 0:CW], ACT.Copy)
                return act.activation(to[:, 2 * CW:N], count_bank(set_, 2), ACT.Copy)

            act.wait_ge(consts, 8)
            clear(0)
            act.wait_ge(ranges, 1)
            act.wait_ge(ecol_sb, 1)
            for what, b in PROLOGUE:
                if what == "counts":
                    one_hots(b)
                    if b == 1:
                        act.wait_ge(ld_w1, 16)
                        for k in range(KD):
                            split_w1(k)
                    if 2 <= b < NB - 1:
                        split_h(0, b - 2, b % 2)
                    if b == 0:
                        counts_out(0)
                    elif 2 <= b < NB - 1:
                        counts_out(b - 1)
                        clear(b + 1)
                elif what == "x":
                    steps(act, NB, 3, 1, split_xT, 3)
                    act.wait_ge(xt_hi, NB)
                    act.wait_ge(xt_lo, NB)
                    act.wait_ge(ecol_sb, 1)
                    clear(1)
                    clear(2)
                elif what == "fold" and b == 2 * KD - 1:
                    act.wait_ge(wa_done, 2 * H * KD)
                    act.activation(wahi[:], wa_f[:], ACT.Copy).then_inc(wa_hi, 1)
                elif what == "scores":
                    if b == 0:
                        split_h(0, NB - 3, 1)
                    for c in (range(2) if b == 0 else (2,)):
                        act.wait_ge(rows_ps, c + 1)
                        act.activation(rows[:, TCH[c][0] * B:TCH[c][1] * B],
                                       PS[0:2 * H, c % 2, 0:(TCH[c][1] - TCH[c][0]) * B], ACT.Copy).then_inc(rows_sb, 1)
                    if b == 1:
                        act.wait_ge(al_ps, 1)
                        act.activation(al[:], PS[0:B, 1, 0:2 * H * NB].rearrange("p (b v) -> p v b", v=2 * H), ACT.Copy
                                       ).then_inc(al_sb, 1)
                        counts_out(NB - 2)
                        act.wait_ge(bc_ps, 1)
                        act.wait_ge(xT_stored, 32 * NB)
                        row_out(arow[:, H - 1, :], 0).then_inc(bc_sb, 1)

            def scores(h, b, s):
                act_scores(act, s, prow, arow[:, H - 1 - h, :], al[:, H + h, bass.ds(b, 1)])

            act.wait_ge(al_sb, 1)
            act.wait_ge(bc_sb, 1)
            scores(0, 0, 0)
            scores(0, 1, 1)
            counts_out(NB - 1)
            act_exp(act, 0, 0, prow)
            act_exp(act, 1, 1, prow)
            split_h(0, NB - 2, 0)
            split_h(0, NB - 1, 1)
            for h in range(1, H):
                act.wait_ge(bc_ps, h + 1)
                row_out(arow[:, H - 1 - h, :], h % 2).then_inc(bc_sb, 1)
            act_split(act, 0, 0, PThi)
            scores(0, 2, 0)
            act_exp(act, 2, 0, prow)
            act_split(act, 1, 1, PThi)
            scores(0, 3, 1)

            for h in range(H):
                def step(j, s):
                    g = NB * h + j
                    more = lambda n: not (h == H - 1 and isinstance(j, int) and j + n >= NB)
                    nxt = lambda n: (h + 1, j + n - NB) if isinstance(j, int) and j + n >= NB else (h, j + n)
                    if more(3):
                        act_exp(act, g + 3, 1 - s, prow)
                    last = isinstance(j, int) and j == NB - 1
                    if more(2) and not last:
                        act.wait_ge(mm_done, 2 * NB * h + NB + j + 1)
                        act_split(act, g + 2, s, PThi)
                    act.wait_ge(v_done, g + 1)
                    if not (isinstance(j, int) and j < 2 and h == 0):
                        act.wait_ge(hid_stored[s], stored(h, j, s))
                    act.activation(ebuf[:, s, :], vbuf[:, s, :], ACT.Exp).then_inc(ex_done, 1)
                    if h + 1 < H and not (isinstance(j, int) and j >= KD):
                        split_w1_of(h + 1, j)
                    if more(4) and not last:
                        act.wait_ge(t_done, g + 3)
                        scores(nxt(4)[0], nxt(4)[1], s)

                def stored(h, j, s):
                    return 16 * (NB // 2) * h + 8 * (j - s)

                def split_w1_of(h1, k):
                    if isinstance(k, int) and k == 0:
                        act.wait_ge(ld_w1, 16 * (h1 + 1))
                        act.wait_ge(mm_done, 2 * NB * (h1 - 1) + NB)
                    split_w1(k)
                steps(act, NB, 2, 4, step)
                if h + 1 < H:
                    steps(act, NB, 0, 0, lambda j, s: split_h(h + 1, j, s))
                    act_split(act, NB * (h + 1) + 1, 1, PThi)
                    scores(h + 1, 3, 1)

            def split_hT(n, b, half):
                if not (isinstance(b, int) and b == 0):
                    act.wait_ge(h2_ps, n - 1)
                act.wait_ge(ht_ps, n + 1)
                act.activation(hThi[:, half, :, :].rearrange("p (a k) n -> p a (k n)", a=2),
                               PS[:, 4 + 2 * half:6 + 2 * half, 0:4 * B], ACT.Copy).then_inc(ht_hi, 1)

            def h2_out(b, s):
                act.wait_ge(h2_ps, 2 * b + 2)
                act.activation(h2f[:, bass.ds(b, 1), :].rearrange("p o (a n) -> p (o a) n", a=2),
                               PS[0:B, 2 * s:2 * s + 2, 0:DH], ACT.Copy).then_inc(h2_sb, 1)

            split_hT(0, 0, 0)
            for c in range(KC):
                act.wait_ge(ld_w2[c % 3], 16 * (c // 3 + 1))
                act.activation(W2hi[:, c, :], w2raw[:, c % 3, :], ACT.Copy).then_inc(w2_hi, 1)
                if c == 2:
                    split_hT(1, 0, 1)

            def h2_step(b, s):
                split_hT(2 * b + 2, b + 1, 0)
                split_hT(2 * b + 3, b + 1, 1)
                h2_out(b, s)
            steps(act, NB, 2, 2, lambda b, s: h2_step(b, s) if not (isinstance(b, int) and b == NB - 1) else h2_out(b, s))

            act.wait_ge(h2_ps, 2 * NB)
            act.wait_ge(h2_sb, NB)

            def split_h2(b, s):
                act.activation(h2hi[:, bass.ds(b, 1), :], h2f[:, bass.ds(b, 1), :], ACT.Copy).then_inc(h2_hi, 1)

            def scores2(b, s):
                act_scores(act, s, prow2, arow2[:], al2[:, 1, bass.ds(b, 1)])
            G2 = H * NB
            split_h2(0, 0)
            split_h2(1, 1)
            act.wait_ge(bc2_ps, 1)
            row_out(arow2, 1).then_inc(bc2_sb, 1)
            act.wait_ge(bc2_sb, 1)
            scores2(0, 0)
            scores2(1, 1)
            act_exp(act, G2, 0, prow2)
            act_exp(act, G2 + 1, 1, prow2)
            act_split(act, G2, 0, PT2hi)
            with act.Fori(1, NB // 2) as k:
                for u in range(2):
                    split_h2(2 * k + u, u)
            scores2(2, 0)
            act_exp(act, G2 + 2, 0, prow2)
            act_split(act, G2 + 1, 1, PT2hi)
            scores2(3, 1)

            def step2(j, s):
                g = G2 + j
                more = lambda n: not (isinstance(j, int) and j + n >= NB)
                if more(3):
                    act_exp(act, g + 3, 1 - s, prow2)
                if more(2):
                    act.wait_ge(mm2_done, j + 1)
                    act_split(act, g + 2, s, PT2hi)
                if more(4):
                    act.wait_ge(t_done, g + 3)
                    scores2(j + 4, s)
            steps(act, NB, 0, 4, step2)

        @block.vector
        def _(dve):
            dve.memset(mhalf[:], -0.5).then_inc(consts_v, 1)
            dve.memset(ones1[:], 1.0).then_inc(consts_v, 1)
            dve.wait_ge(ld_edges, 32)
            dve.tensor_copy(dst_f[:], dst_i[:]).then_inc(edges_f, 1)
            dve.tensor_copy(src_f[:], src_i[:]).then_inc(edges_f, 1)
            dve.wait_ge(edges_f, 1)
            dve.tensor_reduce(dmin[:], dst_f[:].rearrange("p u e -> p (u e)"), AX.X, ALU.min).then_inc(plan, 1)
            dve.tensor_reduce(dmax[:], dst_f[:].rearrange("p u e -> p (u e)"), AX.X, ALU.max).then_inc(plan, 1)
            dve.wait_ge(consts, 8)
            dve.wait_ge(plan, 2)
            dve.tensor_scalar(hit[:, 0, :], blk_hi[:], dmin[:], None, ALU.is_gt)
            dve.tensor_scalar(hit[:, 1, :], blk_lo[:], dmax[:], None, ALU.is_le).then_inc(plan, 1)
            dve.wait_ge(plan, 3)
            dve.tensor_tensor(hit[:, 2, :], hit[:, 0, :], hit[:, 1, :], ALU.mult).then_inc(plan, 1)
            dve.wait_ge(plan, 4)
            dve.tensor_scalar(key[:, 0:NB], hit[:, 2, :], pairid[:], None, ALU.mult).then_inc(plan, 1)
            dve.tensor_scalar(key[:, NB:2 * NB], hit[:, 2, :], pairrv[:], None, ALU.mult).then_inc(plan, 1)
            dve.tensor_copy(ident_b[:], ident[:]).then_inc(consts_v, 1)
            dve.wait_ge(ecol_ps, 1)
            dve.tensor_copy(ecol[:].rearrange("p a n -> p (a n)"), PS[0:B, 7, 0:4 * PAIRS]).then_inc(ecol_sb, 1)
            dve.wait_ge(keys_red, 1)
            dve.tensor_scalar(rng_f[:, 3, :], keyr[0:1, NB:2 * NB], -1.0, float(PAIRS), ALU.mult, ALU.add
                              ).then_inc(plan, 1)
            dve.wait_ge(plan, 7)
            dve.tensor_tensor(rng_f[:, 1, :], keyr[0:1, 0:NB], rng_f[:, 3, :], ALU.subtract).then_inc(plan, 1)
            dve.wait_ge(plan, 8)
            dve.tensor_scalar(rng_f[:, 1, :], rng_f[:, 1, :], 1.0, 0.5, ALU.max, ALU.mult).then_inc(plan, 1)
            dve.wait_ge(plan, 9)
            dve.tensor_scalar(rng_f[:, 1, :], rng_f[:, 1, :], 0.25, None, ALU.add).then_inc(plan, 1)
            dve.wait_ge(plan, 10)
            dve.tensor_scalar(rng_f[:, 1, :], rng_f[:, 1, :], 2.0 ** 23, None, ALU.add).then_inc(plan, 1)
            dve.wait_ge(plan, 11)
            dve.tensor_scalar(rng_f[:, 1, :], rng_f[:, 1, :], -2.0 ** 23, None, ALU.add).then_inc(plan, 1)
            dve.wait_ge(plan, 12)
            dve.wait_ge(consts_v, 3)
            dve.tensor_scalar(rng_f[:, 2, :], rng_f[:, 1, :], -2.0, float(PAIRS), ALU.mult, ALU.add
                              ).then_inc(plan, 1)
            dve.wait_ge(plan, 13)
            dve.tensor_tensor(rng_f[:, 0, :], rng_f[:, 2, :], rng_f[:, 3, :], ALU.min).then_inc(plan, 1)
            dve.wait_ge(plan, 14)
            dve.tensor_tensor_scan(rng_f[:, 3, :], ones1[:], rng_f[:, 1, :], 0.0, ALU.mult, ALU.add
                                   ).then_inc(plan, 1)
            dve.wait_ge(plan, 15)
            dve.tensor_tensor(rng_f[:, 2, :], rng_f[:, 3, :], rng_f[:, 1, :], ALU.subtract)
            dve.tensor_scalar(rng_f[:, 4, :], rng_f[:, 3, :], float(SLOTS), float(DSLOTS), ALU.mult, ALU.add
                              ).then_inc(plan, 1)
            dve.wait_ge(plan, 16)
            dve.tensor_copy(rng_i[:], rng_f[:]).then_inc(ranges, 1)

            def split_xT(j, s):
                dve.wait_ge(xt_hi, j + 1)
                p = x_banks(s)
                dve.tensor_tensor(xalo[:, 0:4, bass.ds(j, 1), :].rearrange("p k o n -> p k (o n)"), PS[:, p, 0:4 * B].rearrange("p (k n) -> p k n", k=4),
                                  xahi[:, 0:4, bass.ds(j, 1), :].bitcast(F32).rearrange("p k o n -> p k (o n)"),
                                  ALU.subtract)
                dve.tensor_tensor(xalo[:, 4:6, bass.ds(j, 1), :].rearrange("p k o n -> p k (o n)"), PS[:, p + 1, 0:2 * B].rearrange("p (k n) -> p k n", k=2),
                                  xahi[:, 4:6, bass.ds(j, 1), :].bitcast(F32).rearrange("p k o n -> p k (o n)"),
                                  ALU.subtract).then_inc(xt_lo, 1)

            def split_h(h, j, s):
                dve.wait_ge(h_hi, NB * h + j + 1)
                dve.tensor_tensor(hlo[:, bass.ds(j, 1), :].rearrange("p o c -> p (o c)"), PS[0:B, s, :],
                                  hhi[:, bass.ds(j, 1), :].bitcast(F32).rearrange("p o c -> p (o c)"),
                                  ALU.subtract).then_inc(h_lo, 1)

            def fold(n):
                k, half = n // 2, n % 2
                dve.wait_ge(ld_wk[n % 3], 16 * (n // 3 + 1))
                for i, v in enumerate((2 * half, H + 2 * half, 2 * half + 1, H + 2 * half + 1)):
                    if 4 * n + i >= 2:
                        dve.wait_ge(wa_done, 4 * n + i - 1)
                    dve.tensor_tensor_reduce(out=junk_w[:, i % 2, :], in0=w1raw[:, 2 * (n % 3) + i // 2, :],
                                             in1=attr[:, v, :], scale=1.0, scalar=0.0, op0=ALU.mult, op1=ALU.add,
                                             accum_out=wa_f[:, k, v:v + 1]).then_inc(wa_done, 1)

            def one_hots(b):
                first, count, before = edge_steps(dve, b)
                with dve.Fori(0, count) as i:
                    for v in range(2):
                        pair = at_pair(first, i, v)
                        dve.wait_ge(oh_free, SLOTS * (before + i) + 2 * v + 2 + DSLOTS - SLOTS)
                        for u in range(2):
                            oh = dve.tensor_scalar(oh_src[:, 2 * v + u, :], colid[:], ecol[:, 2 + u, bass.ds(pair, 1)], None,
                                                   ALU.is_equal)
                        oh.then_inc(oh_done, 1)

            dve.wait_ge(ranges, 1)
            dve.wait_ge(ecol_sb, 1)
            for what, b in PROLOGUE:
                if what == "counts":
                    one_hots(b)
                    if 2 <= b < NB - 1:
                        split_h(0, b - 2, b % 2)
                elif what == "x":
                    steps(dve, NB, 3, 1, split_xT, 3)
                    dve.wait_ge(ld_att, 32)
                elif what == "scores" and b == 0:
                    split_h(0, NB - 3, 1)
                elif what == "fold":
                    fold(b)
                    if b == 2 * KD - 1:
                        dve.wait_ge(wa_hi, 1)
                        dve.tensor_tensor(walo[:], wa_f[:], wahi[:].bitcast(F32), ALU.subtract).then_inc(wa_lo, 1)

            def maxima(h, b):
                dve_max(dve, NB * h + b, b, arow[:, H - 1 - h, :], nbr, junk, al[:, H + h, bass.ds(b, 1)])

            dve.wait_ge(xT_stored, 32 * NB)
            dve.wait_ge(al_sb, 1)
            dve.wait_ge(bc_sb, 1)
            dve.wait_ge(c_done, 4)
            maxima(0, 0)
            dve_leaky(dve, 0, 0, prow)
            maxima(0, 1)
            dve_leaky(dve, 1, 1, prow)
            split_h(0, NB - 2, 0)
            split_h(0, NB - 1, 1)
            dve_counts(dve, 0, 0, 0, prow)
            dve_counts(dve, 1, 1, 1, prow)
            maxima(0, 2)
            dve_split(dve, 0, 0, PThi, PTlo)
            dve_leaky(dve, 2, 0, prow)
            maxima(0, 3)
            dve_counts(dve, 2, 2, 0, prow)
            dve_split(dve, 1, 1, PThi, PTlo)
            dve_leaky(dve, 3, 1, prow)
            dve.wait_ge(c_done, NB)
            dve.wait_ge(bc_sb, H)
            dve.wait_ge(ld_b1, 16)

            for h in range(H):
                def step(j, s):
                    g = NB * h + j
                    more = lambda n: not (h == H - 1 and isinstance(j, int) and j + n >= NB)
                    at = lambda n: j + n - NB if isinstance(j, int) and j + n >= NB else j + n
                    dve.wait_ge(mm_done, 2 * NB * h + NB + j + 1)
                    dve.wait_ge(d_done, g + 1)
                    dve.scalar_tensor_tensor(vbuf[:, s, :], PS[0:B, s, :], rden[:, bass.ds(g, 1)],
                                             b1row[:, h * HC:(h + 1) * HC], ALU.mult, ALU.add).then_inc(v_done, 1)
                    if more(3):
                        dve_counts(dve, g + 3, at(3), 1 - s, prow)
                    last = isinstance(j, int) and j == NB - 1
                    if more(2) and not last:
                        dve_split(dve, g + 2, s, PThi, PTlo)
                    dve.wait_ge(ex_done, g + 1)
                    dve.tensor_scalar(vbuf[:, s, :], vbuf[:, s, :], 0.0, -1.0, ALU.max, ALU.add).then_inc(r_done, 1)
                    dve.wait_ge(r_done, g + 1)
                    dve.scalar_tensor_tensor(ebuf[:, s, :], ebuf[:, s, :], 1.0, vbuf[:, s, :], ALU.min, ALU.add
                                             ).then_inc(hid_done, 1)
                    if more(4) and not last:
                        dve_leaky(dve, g + 4, s, prow)
                    if h == 0 and not isinstance(j, int):
                        maxima(0, j + 4)
                    if h + 1 < H and isinstance(j, int) and 6 <= j < 9:
                        maxima(h + 1, j - 6)
                steps(dve, NB, 0, 4, step)
                if h + 1 < H:
                    def make(j, s):
                        split_h(h + 1, j, s)
                        if not (isinstance(j, int) and j >= NB - 3):
                            maxima(h + 1, j + 3)
                    steps(dve, NB, 0, 4, make)
                    dve_split(dve, NB * (h + 1) + 1, 1, PThi, PTlo)
                    dve_leaky(dve, NB * (h + 1) + 3, 1, prow)

            def split_hT(n, half):
                dve.wait_ge(ht_hi, n + 1)
                dve.tensor_tensor(hTlo[:, half, :, :].rearrange("p (a k) n -> p a (k n)", a=2),
                                  PS[:, 4 + 2 * half:6 + 2 * half, 0:4 * B],
                                  hThi[:, half, :, :].bitcast(F32).rearrange("p (a k) n -> p a (k n)", a=2),
                                  ALU.subtract).then_inc(ht_lo, 1)

            split_hT(0, 0)
            for c in range(KC):
                dve.wait_ge(w2_hi, c + 1)
                dve.tensor_tensor(W2lo[:, c, :], w2raw[:, c % 3, :], W2hi[:, c, :].bitcast(F32), ALU.subtract
                                  ).then_inc(w2_lo, 1)
                if c == 2:
                    split_hT(1, 1)
            dve.wait_ge(ld_a2, 32)

            def scores2(b, s):
                dve.wait_ge(h2_sb, b + 1)
                if not (isinstance(b, int) and b == 0):
                    dve.wait_ge(al2_done, 2 * b)
                blk = h2f[:, bass.ds(b, 1), :].rearrange("p o n -> p (o n)")
                for v in range(2):
                    dve.scalar_tensor_tensor(a2junk[:, v, :], blk, 1.0, a2row[:, v, :], ALU.mult, ALU.mult,
                                             accum_out=al2[:, v, bass.ds(b, 1)]).then_inc(al2_done, 1)

            def h2_step(b, s):
                split_hT(2 * b + 2, 0)
                split_hT(2 * b + 3, 1)
                scores2(b, s)
            steps(dve, NB, 2, 2, lambda b, s: h2_step(b, s) if not (isinstance(b, int) and b == NB - 1) else scores2(b, s))

            G2 = H * NB

            def maxima2(b):
                dve_max(dve, G2 + b, b, arow2[:], nbr2, junk2, al2[:, 1, bass.ds(b, 1)])

            def split_h2(b, s):
                dve.wait_ge(h2_hi, b + 1)
                dve.tensor_tensor(h2lo[:, bass.ds(b, 1), :], h2f[:, bass.ds(b, 1), :],
                                  h2hi[:, bass.ds(b, 1), :].bitcast(F32), ALU.subtract).then_inc(h2_lo, 1)
            split_h2(0, 0)
            split_h2(1, 1)
            dve.wait_ge(bc2_sb, 1)
            maxima2(0)
            dve_leaky(dve, G2, 0, prow2)
            maxima2(1)
            dve_leaky(dve, G2 + 1, 1, prow2)
            dve_counts(dve, G2, 0, 0, prow2)
            dve_counts(dve, G2 + 1, 1, 1, prow2)
            dve_split(dve, G2, 0, PT2hi, PT2lo)
            with dve.Fori(1, NB // 2) as k:
                for u in range(2):
                    split_h2(2 * k + u, u)
            maxima2(2)
            dve_leaky(dve, G2 + 2, 0, prow2)
            maxima2(3)
            dve_counts(dve, G2 + 2, 2, 0, prow2)
            dve_split(dve, G2 + 1, 1, PT2hi, PT2lo)
            dve_leaky(dve, G2 + 3, 1, prow2)
            dve.wait_ge(ld_b2, 16)

            def step2(j, s):
                g = G2 + j
                more = lambda n: not (isinstance(j, int) and j + n >= NB)
                yb = y[:, bass.ds(j, 1), :]
                y2 = yb.rearrange("p o (a n) -> p (o a) n", a=2)
                y1 = yb.rearrange("p o n -> p (o n)")
                banks = PS[0:B, 0:2, 0:DH] if s == 0 else PS[0:B, 5:7, 0:DH]
                dve.wait_ge(mm2_done, j + 1)
                dve.wait_ge(d_done, g + 1)
                dve.scalar_tensor_tensor(y2, banks, rden[:, bass.ds(g, 1)],
                                         b2row[:].rearrange("p (a n) -> p a n", a=2), ALU.mult, ALU.add
                                         ).then_inc(y_b, 1)
                if more(3):
                    dve_counts(dve, g + 3, j + 3, 1 - s, prow2)
                if more(2):
                    dve_split(dve, g + 2, s, PT2hi, PT2lo)
                dve.wait_ge(y_b, j + 1)
                dve.wait_ge(ld_xres[s], xres_loaded(j, s))
                dve.tensor_tensor(y1, y1, xres[:, s, :], ALU.add).then_inc(y_x, 1)
                dve.wait_ge(ld_b2, 16)
                dve.wait_ge(y_x, j + 1)
                for a in range(2):
                    last = dve.bn_stats(bnst[:, a, :], y1[:, a * DH:(a + 1) * DH])
                last.then_inc(y_st, 1)
                if more(4):
                    maxima2(j + 4)
                dve.wait_ge(ld_b2, 16)
                dve.wait_ge(y_st, j + 1)
                dve.bn_aggr(mv[:],
                            bnst[:].rearrange("p a n -> p (a n)")).then_inc(y_mv, 1)
                dve.wait_ge(y_mv, j + 1)
                dve.tensor_scalar(vpe[:], mv[:, 1:2], EPS, None, ALU.add
                                  ).then_inc(y_var, 1)
                if more(4):
                    dve_leaky(dve, g + 4, s, prow2)
                dve.wait_ge(y_pow, j + 1)
                dve.tensor_scalar(y1, y1, mv[:, 0:1],
                                  rstd[:, bass.ds(j, 1)], ALU.subtract, ALU.mult).then_inc(y_done, 1)

            def xres_loaded(j, s):
                return 8 * (j - s) + 16
            steps(dve, NB, 0, 4, step2)

        @block.tensor
        def _(pe):
            pe.wait_ge(consts, 8)
            pe.wait_ge(edges_f, 2)
            for n in range(4):
                t = pe.transpose(PS[0:B, 7, n * PAIRS:(n + 1) * PAIRS], (dst_f, src_f)[n // 2][:, n % 2, :],
                                 ident[0:PAIRS, 0:PAIRS])
            t.then_inc(ecol_ps, 1)

            def transpose_x(j, s):
                if j % XL == 0:
                    pe.wait_ge(ld_x[j // XL], 16)
                if j == 2:
                    pe.wait_ge(c_done, 1)
                if j >= 3:
                    pe.wait_ge(xt_lo, j - 2)
                p = x_banks(s)
                for k in range(KD):
                    t = pe.transpose(PS[:, p + k // 4, (k % 4) * B:(k % 4 + 1) * B],
                                     xall[:, j, k * 128:(k + 1) * 128],
                                     ident[0:B, 0:B])
                t.then_inc(xt_ps, 1)

            def products(dst, parts, start, stop):
                (ahi, alo), (bhi, blo) = parts
                pe.matmul(dst, ahi, bhi, start=start, stop=False)
                pe.matmul(dst, ahi, blo, start=False, stop=False)
                return pe.matmul(dst, alo, bhi, start=False, stop=stop)

            def h_block(j):
                if j == 0:
                    pe.wait_ge(xt_lo, NB)
                    pe.wait_ge(w1_hi, KD)
                    pe.wait_ge(w1_lo, KD)
                if j >= 2:
                    pe.wait_ge(h_lo, j - 1)
                for k in range(KD):
                    t = products(PS[0:B, j % 2, :], ((xahi[:, k, j, :], xalo[:, k, j, :]), (W1hi[:, k, :], W1lo[:, k, :])),
                                 k == 0, k == KD - 1)
                t.then_inc(mm_done, 1)

            def counts(b):
                s = b % 2
                pe.wait_ge(zeroed, b + 1)
                t = pe.matmul(PS[0:B, 2 + 3 * s + b // BB, (b % BB) * B:(b % BB + 1) * B], ident_b[0:B, 0:B],
                              ident_b[0:B, 0:B], start=False, stop=False, skip_group_check=True)
                if b == 0:
                    t.then_inc(oh_free, DSLOTS)
                _, count, before = edge_steps(pe, b)
                with pe.Fori(0, count) as i:
                    turn = (before + i) % 2
                    for v in range(2):
                        pe.wait_ge(oh_done, 2 * (before + i) + v + 1)
                        pe.wait_ge(ohd_done, 2 * (before + i) + v + 1)
                        for slot in (2 * v, 2 * v + 1):
                            for c, (lo, hi) in enumerate(TCH):
                                t = pe.matmul(count_bank(s, c),
                                              oh_dst[:, bass.ds(turn, 1), slot, :].rearrange("p o n -> p (o n)"), oh_src[:, slot, lo * B:hi * B],
                                              start=False, stop=False, skip_group_check=True)
                        t.then_inc(oh_free, 2)

            def score_rows(c):
                lo, hi = TCH[c]
                for k in range(KD):
                    t = products(PS[0:2 * H, c % 2, 0:(hi - lo) * B],
                                 ((wahi[:, k, :], walo[:, k, :]), (xahi[:, k, lo:hi, :].rearrange("p b n -> p (b n)"),
                                   xalo[:, k, lo:hi, :].rearrange("p b n -> p (b n)"))),
                                 k == 0, k == KD - 1)
                t.then_inc(rows_ps, 1)

            def spread(col, set_):
                for b in range(NB):
                    t = pe.matmul(PS[0:B, 2 + 3 * set_ + b // BB, (b % BB) * B:(b % BB + 1) * B],
                                  col(b).broadcast_to([B, B]), ident[0:B, 0:B], start=True, stop=True)
                return t

            pe.wait_ge(ranges, 1)
            pe.wait_ge(consts_v, 3)
            for what, b in PROLOGUE:
                if what == "counts":
                    counts(b)
                elif what == "x":
                    pe.wait_ge(ecol_sb, 1)
                    for j in range(NB):
                        transpose_x(j, j % 3)
                elif what == "h":
                    h_block(b)
                elif what == "scores" and b == 0:
                    pe.wait_ge(h_lo, NB - 2)
                    pe.wait_ge(wa_hi, 1)
                    pe.wait_ge(wa_lo, 1)
                    score_rows(0)
                    score_rows(1)
                elif what == "scores":
                    pe.wait_ge(rows_sb, 2)
                    score_rows(2)
                    pe.wait_ge(rows_sb, 3)
                    for j in range(NB):
                        t = pe.transpose(PS[0:B, 1, 2 * H * j:2 * H * (j + 1)], rows[:, j * B:(j + 1) * B],
                                         ident[0:2 * H, 0:2 * H])
                    t.then_inc(al_ps, 1)
                    pe.wait_ge(al_sb, 1)
                    pe.wait_ge(c_done, NB - 1)
                    spread(lambda b: al[:, 0, b:b + 1], 0).then_inc(bc_ps, 1)
            h_block(NB - 2)
            h_block(NB - 1)
            pe.wait_ge(c_done, NB)
            for h in range(1, H):
                if h >= 2:
                    pe.wait_ge(bc_sb, h - 1)
                spread(lambda b: al[:, h, b:b + 1], h % 2).then_inc(bc_ps, 1)

            pe.wait_ge(bc_sb, 3)
            pe.wait_ge(pc_done, 1)
            pe_transpose(pe, 0, 0, prow)

            for h in range(H):
                def step(j, s):
                    g = NB * h + j
                    if not (h == H - 1 and isinstance(j, int) and j == NB - 1):
                        pe.wait_ge(pc_done, g + 2)
                        pe.wait_ge(pt_lo, g + 1)
                        pe_transpose(pe, g + 1, 1 - s, prow)
                    else:
                        pe.wait_ge(pt_lo, g + 1)
                    if isinstance(j, int) and j < 2:
                        pe.wait_ge(h_lo, NB * (h + 1))
                    else:
                        pe.wait_ge(v_done, g - 1)
                    for b in range(NB):
                        t = products(PS[0:B, s, :], ((PThi[:, s, b, :], PTlo[:, s, b, :]), (hhi[:, b, :], hlo[:, b, :])),
                                     b == 0, b == NB - 1)
                    t.then_inc(mm_done, 1)
                steps(pe, NB, 2, 2, step)
                if h + 1 < H:
                    def make(j, s):
                        if isinstance(j, int) and j < 2:
                            pe.wait_ge(w1_hi, KD * (h + 2))
                            pe.wait_ge(w1_lo, KD * (h + 2))
                            pe.wait_ge(v_done, NB * (h + 1) - 1 + j)
                        else:
                            pe.wait_ge(h_lo, NB * (h + 1) + j - 1)
                        pe.wait_ge(ld_xr[s], 16 * (NB // 2) * h + 8 * (j - s) + 16)
                        for k in range(KD):
                            t = products(PS[0:B, s, :],
                                         ((xr[:, s, 0, k * B:(k + 1) * B], xr[:, s, 1, k * B:(k + 1) * B]),
                                          (W1hi[:, k, :], W1lo[:, k, :])), k == 0, k == KD - 1)
                        t.then_inc(mm_done, 1)
                    steps(pe, NB, 2, 0, make)

            pe.wait_ge(v_done, H * NB)

            def transpose_h(b, s, half):
                if half == 0:
                    pe.wait_ge(ld_hb[s], 8 * (b - s) + 16)
                if not (isinstance(b, int) and b == 0):
                    pe.wait_ge(ht_lo, 2 * b + half - 1)
                for k in range(KH):
                    t = pe.transpose(PS[:, 4 + 2 * half + k // 4, (k % 4) * B:(k % 4 + 1) * B],
                                     hblk[:, s, (half * KH + k) * 128:(half * KH + k + 1) * 128], ident[0:B, 0:B])
                t.then_inc(ht_ps, 1)

            def mm_half(b, s, half):
                pe.wait_ge(ht_lo, 2 * b + half + 1)
                for k in range(KH):
                    c = half * KH + k
                    if isinstance(b, int) and b == 0:
                        pe.wait_ge(w2_lo, c + 1)
                    for a in range(2):
                        t = products(PS[0:B, 2 * s + a, 0:DH],
                                     ((hThi[:, half, k, :], hTlo[:, half, k, :]),
                                      (W2hi[:, c, a * DH:(a + 1) * DH], W2lo[:, c, a * DH:(a + 1) * DH])),
                                     c == 0, c == KC - 1)
                t.then_inc(h2_ps, 1)

            transpose_h(0, 0, 0)
            transpose_h(0, 0, 1)

            def h2_block(b, s):
                if not (isinstance(b, int) and b < 2):
                    pe.wait_ge(h2_sb, b - 1)
                mm_half(b, s, 0)
                if not (isinstance(b, int) and b == NB - 1):
                    transpose_h(b + 1, 1 - s, 0)
                mm_half(b, s, 1)
                if not (isinstance(b, int) and b == NB - 1):
                    transpose_h(b + 1, 1 - s, 1)
            steps(pe, NB, 2, 2, h2_block)
            pe.wait_ge(al2_done, 2 * NB)
            spread(lambda b: al2[:, 0, b:b + 1], 1).then_inc(bc2_ps, 1)

            G2 = H * NB
            pe.wait_ge(bc2_sb, 1)
            pe.wait_ge(h2_sb, NB)
            pe.wait_ge(pc_done, G2 + 1)
            pe_transpose(pe, G2, 0, prow2)

            def step2(j, s):
                g = G2 + j
                if not (isinstance(j, int) and j == NB - 1):
                    pe.wait_ge(pc_done, g + 2)
                    pe.wait_ge(pt_lo, g + 1)
                    pe_transpose(pe, g + 1, 1 - s, prow2)
                else:
                    pe.wait_ge(pt_lo, g + 1)
                if not (isinstance(j, int) and j < 2):
                    pe.wait_ge(y_b, j - 1)
                for b in range(NB):
                    if isinstance(j, int) and j == 0:
                        pe.wait_ge(h2_lo, b + 1)
                    for a in range(2):
                        t = products(PS[0:B, 5 * s + a, 0:DH],
                                     ((PT2hi[:, s, b, :], PT2lo[:, s, b, :]),
                                      (h2hi[:, b, a * DH:(a + 1) * DH], h2lo[:, b, a * DH:(a + 1) * DH])),
                                     b == 0, b == NB - 1)
                t.then_inc(mm2_done, 1)
            steps(pe, NB, 2, 2, step2)


_INS = ["x", "src", "dst", "L0_gnn_W1", "L0_gnn_att_src1", "L0_gnn_att_dst1", "L0_gnn_b1",
        "L0_gnn_W2", "L0_gnn_att_src2", "L0_gnn_att_dst2", "L0_gnn_b2"]


def kernel(**inputs):
    import numpy as _np
    import concourse.bacc as _bacc
    from concourse import mybir as _mybir
    from concourse.bass_utils import run_bass_kernel_spmd as _run

    nc = _bacc.Bacc("TRN2", target_bir_lowering=False, num_devices=1)
    arrays, args = {}, []
    for name in _INS:
        a = _np.ascontiguousarray(inputs[name])
        arrays[f"in_{name}"] = a
        args.append(nc.dram_tensor(f"in_{name}", a.shape, _mybir.dt.from_np(a.dtype), kind="ExternalInput").ap())
    args.append(nc.dram_tensor("out_0", (N, D), F32, kind="ExternalOutput").ap())
    gat_kernel(nc, *args)
    r = _run(nc, [arrays], core_ids=[0])
    return r.results[0]["out_0"]
```

```python
from contextlib import ExitStack

import concourse.bass as bass
from concourse import mybir

F32 = mybir.dt.float32
F32R = mybir.dt.float32r
BF16 = mybir.dt.bfloat16
U16 = mybir.dt.uint16
I32 = mybir.dt.int32
ALU = mybir.AluOpType
ACT = mybir.ActivationFunctionType
AX = mybir.AxisListType
RMAX = bass.bass_isa.ReduceOp.max

N = 1250
E = 20000
B = 125
NB = N // B
PAIRS = E // (2 * B)
D = 768
H = 4
HC = 512
KD = D // 128
HID = H * HC
KC = HID // 128
KH = KC // 2
W2E = 6
WR = 3
DH = D // 2
SLOPE = 0.2
UP = 1 / SLOPE - 1
EPS = 1e-5
MASKED = -1.0e30
BANK = 512
BB = 4
CW = BB * B
TCH = [(0, BB), (BB, 2 * BB), (2 * BB, NB)]
GP = 3
SLOTS = 2 * GP
DSLOTS = 2 * SLOTS
STEPS = -(-PAIRS // GP)
XL = 2
XR = 5


def steps(eng, n, front, back, body):
    for j in range(front):
        body(j, j % 2)
    if n - back > front:
        with eng.Fori(front // 2, (n - back) // 2) as k:
            for u in range(2):
                body(2 * k + u, u)
    for j in range(n - back, n):
        body(j, j % 2)


PROLOGUE = ([("counts", 0), ("x", 0), ("counts", 1), ("x", 1), ("counts", 2), ("counts", 3)]
            + [("h", 0), ("h", 1), ("fold", 0), ("fold", 1), ("fold", 2), ("counts", 4), ("h", 2), ("fold", 3)]
            + [("counts", 5), ("h", 3), ("h", 4), ("fold", 4), ("fold", 5), ("fold", 6), ("counts", 6), ("h", 5), ("fold", 7)]
            + [("counts", 7), ("h", 6), ("h", 7), ("fold", 8), ("fold", 9), ("fold", 10), ("counts", 8), ("fold", 11)]
            + [("scores", 0), ("scores", 1), ("counts", 9)])


def gat_kernel(nc, x, src, dst, W1, as1, ad1, b1, W2, as2, ad2, b2, out):
    xT_d = nc.dram_tensor("xT_scratch", (NB, 128, KD * B), F32, kind="Internal").ap()
    hid_d = nc.dram_tensor("hidden_scratch", (N, HID), F32, kind="Internal").ap()

    with ExitStack() as ctx:
        def sem(name):
            return ctx.enter_context(nc.semaphore(name))

        cursor = [((nc.sbuf_base + 31) // 32) * 32]
        top = [cursor[0]]

        def sb(name, shape, dt):
            size = 1
            for s in shape[1:]:
                size *= s
            size *= {F32: 4, F32R: 4, I32: 4, BF16: 2, U16: 2}[dt]
            t = nc.alloc_sbuf_tensor_at(name, shape, dt, offset=cursor[0])
            cursor[0] += ((size + 31) // 32) * 32
            top[0] = max(top[0], cursor[0])
            return t

        C = sb("counts", [B, NB, N], U16)
        ident = sb("ident", [128, 128], F32)
        ident_b = sb("ident_b", [128, 128], BF16)
        colid = sb("colid", [B, N], U16)
        al = sb("al", [B, 2 * H, NB], F32)
        zero = sb("zero", [B, 1], F32)
        one = sb("one", [B, 1], F32)
        negm = sb("negm", [B, (H + 1) * NB], F32)
        expb = sb("expb", [B, (H + 1) * NB], F32)
        al_up = sb("al_up", [B, H, NB], F32)
        al2_up = sb("al2_up", [B, NB], F32)
        rden = sb("rden", [B, (H + 1) * NB], F32)
        mx = sb("mx", [B, 1], F32)
        gate = sb("gate", [B, 1], F32)
        mneg = sb("mneg", [B, 1], F32)
        den = sb("den", [B, 1], F32)
        deps = sb("deps", [B, 1], F32)
        al2 = sb("al2", [B, 2, NB], F32)
        bnst = sb("bnst", [B, 2, 6], F32)
        mv = sb("mv", [B, 2], F32)
        vpe = sb("vpe", [B, 1], F32)
        rstd = sb("rstd", [B, NB], F32)
        mhalf = sb("mhalf", [B, 1], F32)
        base0 = cursor[0]

        W1hi = sb("W1hi", [128, KD, HC], F32R)
        W1lo = sb("W1lo", [128, KD, HC], F32R)
        w1raw = sb("w1raw", [128, KD, HC], F32)
        hhi = sb("hhi", [B, NB, HC], F32R)
        hlo = sb("hlo", [B, NB, HC], F32R)
        base1 = cursor[0]
        cursor[0] = base1 - 2 * NB * HC * 4
        xall = sb("xall", [B, NB, D], F32)

        cursor[0] = base1
        xahi = sb("xahi", [128, KD, NB, B], F32R)
        xalo = sb("xalo", [128, KD, NB, B], F32R)
        base_attr = cursor[0]
        xt_raw = sb("xt_raw", [128, XR, KD * B], F32)
        cursor[0] = base_attr
        rows = sb("rows", [2 * H, N], F32)
        cursor[0] = base_attr
        dst_i = sb("dst_i", [PAIRS, 2, B], I32)
        src_i = sb("src_i", [PAIRS, 2, B], I32)
        dst_f = sb("dst_f", [PAIRS, 2, B], F32)
        src_f = sb("src_f", [PAIRS, 2, B], F32)
        cursor[0] = base_attr
        attr = sb("attr", [128, 2 * H, HC], F32)
        wa_f = sb("wa_f", [128, KD, 2 * H], F32)
        wahi = sb("wahi", [128, KD, 2 * H], F32R)
        walo = sb("walo", [128, KD, 2 * H], F32R)
        junk_w = sb("junk_w", [128, 2, HC], BF16)
        blk_lo = sb("blk_lo", [PAIRS, NB], F32)
        blk_hi = sb("blk_hi", [PAIRS, NB], F32)
        pairid = sb("pairid", [PAIRS, 1], F32)
        pairrv = sb("pairrv", [PAIRS, 1], F32)
        dmin = sb("dmin", [PAIRS, 1], F32)
        dmax = sb("dmax", [PAIRS, 1], F32)
        hit = sb("hit", [PAIRS, 3, NB], F32)
        key = sb("key", [PAIRS, 2 * NB], F32)
        keyr = sb("keyr", [PAIRS, 2 * NB], F32)
        rng_f = sb("rng_f", [1, 5, NB], F32)
        ones1 = sb("ones1", [1, NB], F32)
        prologue_end = cursor[0]

        cursor[0] = base1
        PThi = sb("PThi", [B, 2, NB, B], F32R)
        PTlo = sb("PTlo", [B, 2, NB, B], F32R)
        xr = sb("xr", [128, 2, 2, KD * B], F32R)
        b1row = sb("b1row", [B, HID], F32)
        vbuf = sb("vbuf", [B, 2, HC], F32)
        ebuf = sb("ebuf", [B, 2, HC], F32)
        arow_at = cursor[0]
        arow = sb("arow", [B, H, N], F32)
        assert cursor[0] - N * 4 >= base1 + 2 * NB * KD * B * 4
        prow = sb("prow", [B, 2, N], F32)
        heads_last = cursor[0]
        nbr = sb("nbr", [B, N], BF16)
        heads_part = cursor[0]
        cursor[0] = max(prologue_end, heads_part)
        oh_src = sb("oh_src", [B, SLOTS, N], BF16)
        oh_dst = sb("oh_dst", [B, 2, SLOTS, B], BF16)
        oh_sq = sb("oh_sq", [B, 2, GP, 2, B], BF16)
        ecol = sb("ecol", [B, 4, PAIRS + GP - 1], F32)
        rng_i = sb("rng_i", [1, 5, NB], I32)
        cursor[0] = heads_part
        xf = sb("xf", [128, 2, KD * B], F32)

        cursor[0] = base0
        W2p = sb("W2p", [128, KC, 2, D], F32R)
        assert base0 + W2E * 2 * D * 4 <= base0 + 3 * KD * HC * 4
        w2late = sb("w2late", [128, KC - 3 * WR, D], F32)
        cursor[0] = base0 + 2 * KC * D * 4
        h2f = sb("h2f", [B, NB, D], F32)
        base2 = cursor[0]
        cursor[0] = (arow_at + N * 4 + 31) // 32 * 32
        assert base2 <= cursor[0] and cursor[0] + 2 * KH * B * 4 <= arow_at + H * N * 4
        hT = sb("hT", [128, 2, 2, KH, B], F32R)
        a2row = sb("a2row", [B, 2, D], F32)
        a2junk = sb("a2junk", [B, 2, D], BF16)
        cursor[0] = max(cursor[0], heads_last)
        w2raw = sb("w2raw", [128, WR, D], F32)
        hblk = sb("hblk", [B, 2, HID], F32)

        cursor[0] = base0
        h2hi = sb("h2hi", [B, NB, D], F32R)
        h2lo = sb("h2lo", [B, NB, D], F32R)
        prow2 = sb("prow2", [B, 2, N], F32)
        PT2hi = sb("PT2hi", [B, 2, NB, B], F32R)
        PT2lo = sb("PT2lo", [B, 2, NB, B], F32R)
        b2row = sb("b2row", [B, D], F32)
        assert cursor[0] <= base0 + 2 * KC * D * 4
        cursor[0] = base2
        arow2 = sb("arow2", [B, N], F32)
        assert cursor[0] <= arow_at + N * 4 + 2 * KH * B * 4
        y = sb("y", [B, NB, D], F32)
        xres = sb("xres", [B, 2, D], F32)
        nbr2 = sb("nbr2", [B, N], BF16)
        assert top[0] <= nc.sbuf_usable_end, (top[0], nc.sbuf_usable_end)

        PS = ctx.enter_context(nc.psum_tensor("ps", [128, 8, BANK], F32))

        ld_edges = sem("ld_edges")
        ld_x = [sem(f"ld_x{i}") for i in range(NB // XL)]
        ld_w1 = sem("ld_w1")
        ld_att = sem("ld_att")
        ld_wk = [sem(f"ld_wk{i}") for i in range(3)]
        xT_stored = [sem(f"xT_stored{i}") for i in range(XR)]
        ld_b1 = sem("ld_b1")
        ld_xf = [sem(f"ld_xf{i}") for i in range(2)]
        hid_stored = [sem(f"hid_stored{i}") for i in range(2)]
        ld_hb = [sem(f"ld_hb{i}") for i in range(2)]
        ld_a2 = sem("ld_a2")
        ld_w2 = [sem(f"ld_w2{c}") for c in range(KC)]
        ld_b2 = sem("ld_b2")
        ld_xres = [sem(f"ld_xres{i}") for i in range(2)]
        out_stored = sem("out_stored")

        consts = sem("consts")
        consts_v = sem("consts_v")
        edges_f = sem("edges_f")
        ecol_ps = sem("ecol_ps")
        ecol_sb = sem("ecol_sb")
        plan = sem("plan")
        keys_red = sem("keys_red")
        ranges = sem("ranges")
        xt_ps = sem("xt_ps")
        xt_hi = sem("xt_hi")
        xt_lo = sem("xt_lo")
        xt_raw_done = sem("xt_raw_done")
        xr_hi = sem("xr_hi")
        xr_lo = sem("xr_lo")
        w1_hi = sem("w1_hi")
        w1_lo = sem("w1_lo")
        h_hi = sem("h_hi")
        h_lo = sem("h_lo")
        mm_done = sem("mm_done")
        wa_done = sem("wa_done")
        wa_hi = sem("wa_hi")
        wa_lo = sem("wa_lo")
        zeroed = sem("zeroed")
        oh_done = sem("oh_done")
        sq_done = sem("sq_done")
        ohd_done = sem("ohd_done")
        oh_free = sem("oh_free")
        c_done = sem("c_done")
        rows_ps = sem("rows_ps")
        rows_sb = sem("rows_sb")
        al_ps = sem("al_ps")
        al_sb = sem("al_sb")
        bc_ps = sem("bc_ps")
        bc_sb = sem("bc_sb")
        mask_done = sem("mask_done")
        max_done = sem("max_done")
        mneg_done = sem("mneg_done")
        negm_done = sem("negm_done")
        up_sb = sem("up_sb")
        m_done = sem("m_done")
        z_done = sem("z_done")
        e_done = sem("e_done")
        p_done = sem("p_done")
        pc_done = sem("pc_done")
        d_eps = sem("d_eps")
        d_done = sem("d_done")
        t_done = sem("t_done")
        pt_hi = sem("pt_hi")
        pt_lo = sem("pt_lo")
        v_done = sem("v_done")
        neg_done = sem("neg_done")
        ex_done = sem("ex_done")
        hid_done = sem("hid_done")
        w2_hi = sem("w2_hi")
        w2_lo_p = sem("w2_lo_p")
        w2_lo = sem("w2_lo")
        ht_ps = sem("ht_ps")
        ht_hi = sem("ht_hi")
        ht_lo = sem("ht_lo")
        h2_ps = sem("h2_ps")
        h2_sb = sem("h2_sb")
        al2_done = sem("al2_done")
        bc2_ps = sem("bc2_ps")
        bc2_sb = sem("bc2_sb")
        h2_hi = sem("h2_hi")
        h2_lo = sem("h2_lo")
        mm2_done = sem("mm2_done")
        y_b = sem("y_b")
        xb_done = sem("xb_done")
        y_st = sem("y_st")
        y_mv = sem("y_mv")
        y_var = sem("y_var")
        y_pow = sem("y_pow")
        y_done = sem("y_done")

        def count_bank(s, c):
            return PS[0:B, 2 + 3 * s + c, 0:(TCH[c][1] - TCH[c][0]) * B]

        def x_banks(j):
            return (0, 5 if j < NB // 2 else 2)[j % 2]

        block = ctx.enter_context(nc.Block())

        def w2_raw(c):
            return w2raw[:, c % WR, :] if c < 3 * WR else w2late[:, c - 3 * WR, :]

        def w2_lo_done(eng, c):
            if c < W2E:
                eng.wait_ge(w2_lo_p, c + 1)
            else:
                eng.wait_ge(w2_lo, c - W2E + 1)

        def h2_banks(s):
            return PS[0:B, 2 - 2 * s:4 - 2 * s, 0:DH]

        def w2_early(j):
            return {6: (0, 1), 7: (2, 3), 8: (4, 5)}.get(j, ())

        def ht_banks(half):
            return ((5, 6), (4, 7))[half]

        def ht_part(half, part, a):
            return hT[:, half, part, a * KH // 2:(a + 1) * KH // 2, :].rearrange("p k n -> p (k n)")

        def edge_steps(eng, b):
            return (eng.value_load(rng_i[0:1, 0, b:b + 1], min_val=0, max_val=PAIRS - 1),
                    eng.value_load(rng_i[0:1, 1, b:b + 1], min_val=1, max_val=STEPS),
                    eng.value_load(rng_i[0:1, 2, b:b + 1], min_val=0, max_val=NB * STEPS))

        def at_pair(first, i, v):
            return nc.s_assert_within(first + GP * i + v, 0, PAIRS + GP - 2,
                                      skip_runtime_bounds_check_because="a block's steps end with the padding")

        def act_relu(act, s, buf, row, up_dst):
            act.activation(buf[:, s, :], row, ACT.Relu, scale=UP, bias=up_dst).then_inc(z_done, 1)

        def pool_add(pool, g, s, buf, row):
            pool.wait_ge(z_done, g + 1)
            pool.tensor_tensor(buf[:, s, :], buf[:, s, :], row, ALU.add).then_inc(e_done, 1)

        def act_exp(act, g, s, buf):
            act.wait_ge(e_done, g + 1)
            act.wait_ge(m_done, g + 1)
            act.activation(buf[:, s, :], buf[:, s, :], ACT.Exp, scale=SLOPE, bias=expb[:, bass.ds(g, 1)]
                           ).then_inc(p_done, 1)

        def act_split(act, g, s, hi):
            act.wait_ge(t_done, g + 1)
            act.activation(hi[:, s, 0:8, :].rearrange("p (a b) n -> p a (b n)", a=2),
                           PS[0:B, 2:4, 0:4 * B], ACT.Copy)
            act.activation(hi[:, s, 8:10, :].rearrange("p b n -> p (b n)"),
                           PS[0:B, 4, 0:2 * B], ACT.Copy).then_inc(pt_hi, 1)

        def dve_max(dve, g, b, row, scr, dcol):
            dve.tensor_scalar(scr[:], C[:, bass.ds(b, 1), :].rearrange("p o n -> p (o n)"), 0.0, MASKED,
                              ALU.is_equal, ALU.mult).then_inc(mask_done, 1)
            dve.wait_ge(mask_done, g + 1)
            dve.memset(gate[:], 0.0)
            dve.tensor_tensor_reduce(out=scr[:], in0=scr[:], in1=row, scale=1.0, scalar=-3.0e38,
                                     op0=ALU.add, op1=ALU.max, accum_out=mx[:]).then_inc(max_done, 1)
            dve.wait_ge(max_done, g + 1)
            dve.scalar_tensor_tensor(mneg[:], mx[:], -1.0, dcol, ALU.mult, ALU.subtract).then_inc(mneg_done, 1)
            dve.wait_ge(mneg_done, g + 1)
            dve.scalar_tensor_tensor(negm[:, bass.ds(g, 1)], mneg[:], SLOPE, mneg[:], ALU.mult, ALU.min
                                     ).then_inc(negm_done, 1)
            dve.wait_ge(negm_done, g + 1)
            dve.scalar_tensor_tensor(expb[:, bass.ds(g, 1)], dcol, SLOPE, negm[:, bass.ds(g, 1)], ALU.mult, ALU.add
                                     ).then_inc(m_done, 1)

        def dve_counts(dve, g, b, s, buf):
            dve.wait_ge(p_done, g + 1)
            dve.scalar_tensor_tensor(buf[:, s, :], buf[:, s, :], 1.0,
                                     C[:, bass.ds(b, 1), :].rearrange("p o n -> p (o n)"),
                                     ALU.min, ALU.mult, accum_out=den[:]).then_inc(pc_done, 1)
            dve.wait_ge(pc_done, g + 1)
            dve.tensor_scalar(deps[:], den[:], 1e-16, None, ALU.add).then_inc(d_eps, 1)
            dve.wait_ge(d_eps, g + 1)
            dve.reciprocal(rden[:, bass.ds(g, 1)], deps[:]).then_inc(d_done, 1)

        def dve_split(dve, g, s, hi, lo):
            dve.wait_ge(pt_hi, g + 1)
            dve.tensor_tensor(lo[:, s, 0:8, :].rearrange("p (a b) n -> p a (b n)", a=2), PS[0:B, 2:4, 0:4 * B],
                              hi[:, s, 0:8, :].bitcast(F32).rearrange("p (a b) n -> p a (b n)", a=2), ALU.subtract)
            dve.tensor_tensor(lo[:, s, 8:10, :].rearrange("p b n -> p (b n)"), PS[0:B, 4, 0:2 * B],
                              hi[:, s, 8:10, :].bitcast(F32).rearrange("p b n -> p (b n)"), ALU.subtract
                              ).then_inc(pt_lo, 1)

        def pe_transpose(pe, g, s, buf):
            for bank, (lo, hi) in enumerate(TCH):
                for b in range(lo, hi):
                    t = pe.transpose(PS[0:B, 2 + bank, (b - lo) * B:(b - lo + 1) * B],
                                     buf[:, s, b * B:(b + 1) * B], ident[0:B, 0:B])
            t.then_inc(t_done, 1)

        @block.sync
        def _(sp):
            sp.dma_start(dst_i[:], dst.rearrange("(p u e) -> p u e", u=2, e=B)).then_inc(ld_edges, 16)
            sp.dma_start(src_i[:], src.rearrange("(p u e) -> p u e", u=2, e=B)).then_inc(ld_edges, 16)

            for i in range(NB // XL):
                sp.dma_start(xall[:, XL * i:XL * (i + 1), :], x[XL * i * B:XL * (i + 1) * B, :]
                             .rearrange("(b p) d -> p b d", p=B)).then_inc(ld_x[i], 16)

            def load_w1(h):
                sp.dma_start(w1raw[:], W1[:, h * HC:(h + 1) * HC].rearrange("(k p) c -> p k c", p=128)
                             ).then_inc(ld_w1, 16)

            load_w1(0)
            for j in range(NB):
                sp.wait_ge(xt_raw_done, j + 1)
                sp.dma_start(xT_d[j], xt_raw[:, j % XR, :]).then_inc(xT_stored[j % XR], 16)
            for i in range(XR):
                sp.wait_ge(xT_stored[i], 16 * (NB // XR))
            sp.wait_ge(xt_lo, NB)
            sp.dma_start(attr[:, 0:H, :], as1.rearrange("(o h) c -> o h c", o=1).broadcast_to([128, H, HC])
                         ).then_inc(ld_att, 16)
            sp.dma_start(attr[:, H:2 * H, :], ad1.rearrange("(o h) c -> o h c", o=1).broadcast_to([128, H, HC])
                         ).then_inc(ld_att, 16)

            sp.wait_ge(w1_hi, KD)
            sp.wait_ge(w1_lo, KD)
            for n in range(2 * KD):
                if n >= 3:
                    sp.wait_ge(wa_done, H * (n - 2))
                sp.dma_start(w1raw[:, 2 * (n % 3):2 * (n % 3) + 2, :],
                             W1[128 * (n // 2):128 * (n // 2) + 128, bass.ts(n % 2, 2 * HC)]
                             .rearrange("p (a c) -> p a c", a=2)).then_inc(ld_wk[n % 3], 16)
            sp.wait_ge(wa_done, 2 * H * KD)
            load_w1(1)

            sp.wait_ge(rows_ps, 3)
            sp.wait_ge(mm_done, NB)
            sp.dma_start(b1row[:], b1.rearrange("(o n) -> o n", o=1).broadcast_to([B, HID])).then_inc(ld_b1, 16)

            def load_xf(h, j, s):
                if not (h == 1 and isinstance(j, int) and j < 2):
                    sp.wait_ge(xr_lo, NB * (h - 1) + j - 1)
                sp.dma_start(xf[:, s, :], xT_d[bass.ds(j, 1), :, :].rearrange("o p n -> p (o n)")).then_inc(ld_xf[s], 16)

            def store_hid(h, j, s):
                sp.wait_ge(hid_done, NB * h + j + 1)
                sp.dma_start(hid_d[bass.ds(j * B, B), h * HC:(h + 1) * HC], ebuf[:, s, :]).then_inc(hid_stored[s], 16)

            def load_w2(c):
                if WR <= c < 3 * WR:
                    sp.wait_ge(w2_hi, c - WR + 1)
                    w2_lo_done(sp, c - WR)
                sp.dma_start(w2_raw(c), W2[128 * c:128 * c + 128, :]).then_inc(ld_w2[c], 16)

            def load_hb(b, s):
                if isinstance(b, int) and b < 2:
                    sp.wait_ge(hid_stored[s], 8 * (H - 1) * NB + 16)
                else:
                    sp.wait_ge(ht_ps, 2 * b - 2)
                sp.dma_start(hblk[:, s, :], hid_d[bass.ds(b * B, B), :]).then_inc(ld_hb[s], 16)

            for h in range(H):
                if h == H - 1:
                    sp.wait_ge(m_done, H * NB)
                    sp.wait_ge(xr_lo, NB * (H - 1))
                    for c in range(WR):
                        load_w2(c)
                if h + 1 < H:
                    load_xf(h + 1, 0, 0)
                    load_xf(h + 1, 1, 1)

                def head(j, s):
                    if h == H - 1 and isinstance(j, int) and j == NB - 4:
                        load_hb(0, 0)
                        load_hb(1, 1)
                    if h == H - 1 and isinstance(j, int) and j >= NB - 2:
                        for c in range(WR * (1 + s), WR * (2 + s)):
                            load_w2(c)
                    if h + 1 < H and isinstance(j, int) and j == NB - 2:
                        load_xf(h + 1, 2, 0)
                        load_xf(h + 1, 3, 1)
                    store_hid(h, j, s)
                steps(sp, NB, 0, 4, head)
                if h + 1 < H:
                    with sp.Fori(2, NB // 2) as k:
                        for u in range(2):
                            load_xf(h + 1, 2 * k + u, u)
                if h + 2 < H:
                    sp.wait_ge(w1_hi, KD * (h + 2))
                    sp.wait_ge(w1_lo, KD * (h + 2))
                    load_w1(h + 2)

            sp.wait_ge(mm_done, 2 * H * NB)
            sp.wait_ge(v_done, H * NB)
            for c in range(3 * WR, KC):
                load_w2(c)
            sp.dma_start(a2row[:, 0, :], as2.broadcast_to([B, D])).then_inc(ld_a2, 16)
            sp.dma_start(a2row[:, 1, :], ad2.broadcast_to([B, D])).then_inc(ld_a2, 16)
            for i in range(2):
                sp.wait_ge(hid_stored[i], 16 * H * NB // 2)
            with sp.Fori(1, NB // 2) as k:
                for u in range(2):
                    load_hb(2 * k + u, u)

            sp.wait_ge(al2_done, 2 * NB)
            sp.dma_start(b2row[:], b2.rearrange("(o n) -> o n", o=1).broadcast_to([B, D])).then_inc(ld_b2, 16)

            def load_xres(b, s):
                if not (isinstance(b, int) and b < 2):
                    sp.wait_ge(y_b, b - 1)
                sp.dma_start(xres[:, s, :], x[bass.ds(b * B, B), :]).then_inc(ld_xres[s], 16)

            def store_out(b, s):
                sp.wait_ge(y_done, b + 1)
                sp.dma_start(out[bass.ds(b * B, B), :], y[:, bass.ds(b, 1), :].rearrange("p o n -> p (o n)")
                             ).then_inc(out_stored, 16)

            load_xres(0, 0)
            load_xres(1, 1)
            with sp.Fori(1, NB // 2) as k:
                for u in range(2):
                    load_xres(2 * k + u, u)
                    store_out(2 * k + u - 2, u)
            store_out(NB - 2, 0)
            store_out(NB - 1, 1)
            sp.wait_ge(out_stored, 16 * NB)

        @block.gpsimd
        def _(pool):
            pool.memset(ident[:], 0.0).then_inc(consts, 1)
            pool.iota(colid[:], [[1, N]], base=0, channel_multiplier=0).then_inc(consts, 1)
            pool.memset(zero[:], 0.0)
            pool.memset(one[:], 1.0).then_inc(consts, 1)
            pool.iota(blk_lo[:], [[B, NB]], base=0, channel_multiplier=0,
                      allow_small_or_imprecise_dtypes=True).then_inc(consts, 1)
            pool.iota(blk_hi[:], [[B, NB]], base=B, channel_multiplier=0,
                      allow_small_or_imprecise_dtypes=True).then_inc(consts, 1)
            pool.iota(pairid[:], [[1, 1]], base=1, channel_multiplier=1,
                      allow_small_or_imprecise_dtypes=True).then_inc(consts, 1)
            pool.iota(pairrv[:], [[1, 1]], base=PAIRS, channel_multiplier=-1,
                      allow_small_or_imprecise_dtypes=True).then_inc(consts, 1)
            pool.wait_ge(consts, 7)
            pool.affine_select(out=ident[:], in_=ident[:], compare_op=ALU.not_equal, fill=1.0, base=0,
                               pattern=[[-1, 128]], channel_multiplier=1).then_inc(consts, 1)
            pool.wait_ge(plan, 6)
            pool.partition_all_reduce(keyr[:], key[:], PAIRS, RMAX).then_inc(keys_red, 1)

            def split_w1(h, k):
                pool.wait_ge(w1_hi, KD * h + k + 1)
                pool.tensor_tensor(W1lo[:, bass.ds(k, 1), :], w1raw[:, bass.ds(k, 1), :],
                                   W1hi[:, bass.ds(k, 1), :].bitcast(F32), ALU.subtract).then_inc(w1_lo, 1)

            def split_w2(c):
                pool.wait_ge(w2_hi, c + 1)
                pool.tensor_tensor(W2p[:, c, 1, :], w2_raw(c), W2p[:, c, 0, :].bitcast(F32), ALU.subtract
                                   ).then_inc(w2_lo_p, 1)

            def split_x(h, j, s):
                pool.wait_ge(xr_hi, NB * (h - 1) + j + 1)
                pool.tensor_tensor(xr[:, s, 1, :], xf[:, s, :], xr[:, s, 0, :].bitcast(F32), ALU.subtract).then_inc(xr_lo, 1)

            for k in range(KD):
                split_w1(0, k)

            for j in range(4):
                pool_add(pool, j, j % 2, prow, arow[:, H - 1, :])
            for h in range(H):
                def step(j, s):
                    last = isinstance(j, int) and j == NB - 1
                    if not last and not (h == H - 1 and isinstance(j, int) and j + 4 >= NB):
                        nh = h + 1 if isinstance(j, int) and j + 4 >= NB else h
                        pool_add(pool, NB * h + j + 4, s, prow, arow[:, H - 1 - nh, :])
                    if h + 1 < H and not (isinstance(j, int) and j >= KD):
                        split_w1(h + 1, j)
                    if h + 1 < H and isinstance(j, int) and j in (KD, KD + 1):
                        split_x(h + 1, j - KD, s)
                    if h == H - 1 and isinstance(j, int):
                        for c in w2_early(j):
                            split_w2(c)
                steps(pool, NB, 0, 4, step)
                if h + 1 < H:
                    with pool.Fori(1, NB // 2) as k:
                        for u in range(2):
                            split_x(h + 1, 2 * k + u, u)
                    pool_add(pool, NB * (h + 1) + 3, 1, prow, arow[:, H - 2 - h, :])

            def pow_var(b, s):
                pool.wait_ge(y_var, b + 1)
                pool.tensor_tensor(rstd[:, bass.ds(b, 1)], vpe[:], mhalf[:], ALU.pow).then_inc(y_pow, 1)
            for j in range(4):
                pool_add(pool, H * NB + j, j % 2, prow2, arow2[:])

            def add_bias(b, s):
                pool.wait_ge(ld_xres[s], 8 * (b - s) + 16)
                pool.tensor_tensor(xres[:, s, :], xres[:, s, :], b2row[:], ALU.add).then_inc(xb_done, 1)

            pool.wait_ge(ld_b2, 16)
            add_bias(0, 0)

            def step2(j, s):
                pow_var(j, s)
                if not (isinstance(j, int) and j == NB - 1):
                    add_bias(j + 1, 1 - s)
                if not isinstance(j, int):
                    pool_add(pool, H * NB + j + 4, s, prow2, arow2[:])
            steps(pool, NB, 0, 4, step2)

        @block.scalar
        def _(act):
            def copy_xT(j):
                act.wait_ge(xt_ps, j + 1)
                if j >= XR:
                    act.wait_ge(xT_stored[j % XR], 16 * (j // XR))
                    act.wait_ge(xt_lo, j - XR + 1)
                p, r = x_banks(j), j % XR
                act.activation(xt_raw[:, r, 0:4 * B], PS[:, p, 0:4 * B], ACT.Copy)
                act.activation(xt_raw[:, r, 4 * B:KD * B], PS[:, p + 1, 0:2 * B], ACT.Copy).then_inc(xt_raw_done, 1)

            def split_x(h, j, s):
                act.wait_ge(ld_xf[s], 16 * (NB // 2) * (h - 1) + 8 * (j - s) + 16)
                if not (isinstance(j, int) and j < 2):
                    act.wait_ge(mm_done, 2 * NB * h + j - 1)
                act.activation(xr[:, s, 0, :], xf[:, s, :], ACT.Copy).then_inc(xr_hi, 1)

            def split_w1(k):
                act.activation(W1hi[:, bass.ds(k, 1), :], w1raw[:, bass.ds(k, 1), :], ACT.Copy).then_inc(w1_hi, 1)

            def split_h(h, j, s):
                act.wait_ge(mm_done, 2 * NB * h + j + 1)
                act.activation(hhi[:, bass.ds(j, 1), :].rearrange("p o c -> p (o c)"), PS[0:B, s, :], ACT.Copy
                               ).then_inc(h_hi, 1)

            def clear(b):
                if b >= 2:
                    act.wait_ge(c_done, b - 1)
                act.activation(PS[0:B, 2 + 3 * (b % 2):5 + 3 * (b % 2), 0:CW],
                               zero[:].rearrange("p (o n) -> p o n", o=1).broadcast_to([B, 3, CW]), ACT.Copy
                               ).then_inc(zeroed, 1)

            def one_hots(b):
                first, count, before = edge_steps(act, b)
                with act.Fori(0, count) as i:
                    turn = (before + i) % 2
                    for v in range(GP):
                        pair = at_pair(first, i, v)
                        half = GP * (before + i) + v
                        sq_v = oh_sq[:, bass.ds(turn, 1), v, :, :].rearrange("p o u n -> p (o u n)")
                        act.wait_ge(oh_free, 2 * half + 2)
                        for u in range(2):
                            sq = act.activation(sq_v[:, u * B:(u + 1) * B], colid[:, b * B:(b + 1) * B], ACT.Square, scale=-1.0,
                                                bias=ecol[:, u, bass.ds(pair, 1)])
                        sq.then_inc(sq_done, 1)
                        act.wait_ge(sq_done, half + 1)
                        act.activation(oh_dst[:, bass.ds(turn, 1), 2 * v:2 * v + 2, :].rearrange("p o u n -> p (o u n)"),
                                       sq_v, ACT.Relu, scale=-1.0, bias=one[:]).then_inc(ohd_done, 1)

            def counts_out(b):
                last = act.value_load(rng_i[0:1, 4, b:b + 1], min_val=SLOTS + DSLOTS, max_val=SLOTS * NB * STEPS + DSLOTS)
                act.wait_ge(oh_free, last)
                s = b % 2
                act.activation(C[:, b, 0:2 * CW].rearrange("p (a n) -> p a n", a=2),
                               PS[0:B, 2 + 3 * s:4 + 3 * s, 0:CW], ACT.Copy)
                act.activation(C[:, b, 2 * CW:N], count_bank(s, 2), ACT.Copy).then_inc(c_done, 1)

            def row_out(to, set_):
                p = 2 + 3 * set_
                act.activation(to[:, 0:2 * CW].rearrange("p (a n) -> p a n", a=2), PS[0:B, p:p + 2, 0:CW], ACT.Copy)
                return act.activation(to[:, 2 * CW:N], count_bank(set_, 2), ACT.Copy)

            act.wait_ge(consts, 8)
            clear(0)
            act.wait_ge(ecol_sb, 1)
            act.wait_ge(consts_v, 4)
            act.wait_ge(ranges, 1)
            made = []
            for what, b in PROLOGUE:
                if what == "counts":
                    one_hots(b)
                    while made:
                        j = made.pop(0)
                        split_h(0, j, j % 2)
                    if 1 <= b < NB - 1:
                        counts_out(b - 1)
                        if b >= 2:
                            clear(b + 1)
                    if b == 2:
                        act.wait_ge(ld_w1, 16)
                        for k in range(KD):
                            split_w1(k)
                elif what == "x":
                    for j in range(NB // 2 * b, NB // 2 * (b + 1)):
                        copy_xT(j)
                    act.wait_ge(xt_raw_done, NB // 2 * (b + 1))
                    clear(b + 1)
                elif what == "h":
                    made.append(b)
                elif what == "fold" and b == 2 * KD - 1:
                    act.wait_ge(wa_done, 2 * H * KD)
                    act.activation(wahi[:], wa_f[:], ACT.Copy).then_inc(wa_hi, 1)
                elif what == "scores":
                    for c in (range(2) if b == 0 else (2,)):
                        act.wait_ge(rows_ps, c + 1)
                        act.activation(rows[:, TCH[c][0] * B:TCH[c][1] * B],
                                       PS[0:2 * H, c % 2, 0:(TCH[c][1] - TCH[c][0]) * B], ACT.Copy).then_inc(rows_sb, 1)
                    if b == 1:
                        act.wait_ge(al_ps, 1)
                        act.activation(al[:], PS[0:B, 1, 0:2 * H * NB].rearrange("p (b v) -> p v b", v=2 * H), ACT.Copy
                                       ).then_inc(al_sb, 1)
                        counts_out(NB - 2)

            def scores(h, b, s):
                act_relu(act, s, prow, arow[:, H - 1 - h, :], al_up[:, h, bass.ds(b, 1)])

            act.wait_ge(al_sb, 1)
            act.activation(al_up[:], al[:, H:2 * H, :], ACT.Copy, scale=UP).then_inc(up_sb, 1)
            act.wait_ge(bc_ps, 1)
            row_out(arow[:, H - 1, :], 0).then_inc(bc_sb, 1)
            act.wait_ge(up_sb, 1)
            act.wait_ge(bc_sb, 1)
            scores(0, 0, 0)
            scores(0, 1, 1)
            counts_out(NB - 1)
            act_exp(act, 0, 0, prow)
            act_exp(act, 1, 1, prow)
            split_h(0, NB - 2, 0)
            split_h(0, NB - 1, 1)
            for h in range(1, H):
                act.wait_ge(bc_ps, h + 1)
                row_out(arow[:, H - 1 - h, :], h % 2).then_inc(bc_sb, 1)
            act_split(act, 0, 0, PThi)
            scores(0, 2, 0)
            act_split(act, 1, 1, PThi)
            scores(0, 3, 1)
            act_exp(act, 2, 0, prow)

            def split_hT(n, b, half):
                if not (isinstance(b, int) and b == 0):
                    act.wait_ge(h2_ps, n - 1)
                act.wait_ge(ht_ps, n + 1)
                for a, bank in enumerate(ht_banks(half)):
                    hi = act.activation(ht_part(half, 0, a), PS[:, bank, 0:4 * B], ACT.Copy)
                hi.then_inc(ht_hi, 1)

            def split_w2(c):
                act.wait_ge(ld_w2[c], 16)
                act.activation(W2p[:, c, 0, :], w2_raw(c), ACT.Copy).then_inc(w2_hi, 1)

            for h in range(H):
                def step(j, s):
                    g = NB * h + j
                    more = lambda n: not (h == H - 1 and isinstance(j, int) and j + n >= NB)
                    nxt = lambda n: (h + 1, j + n - NB) if isinstance(j, int) and j + n >= NB else (h, j + n)
                    last = isinstance(j, int) and j == NB - 1
                    if more(3) and not last:
                        act_exp(act, g + 3, 1 - s, prow)
                    if more(2) and not last:
                        act.wait_ge(mm_done, 2 * NB * h + NB + j + 1)
                        act_split(act, g + 2, s, PThi)
                    act.wait_ge(v_done, g + 1)
                    if not (isinstance(j, int) and j < 2 and h == 0):
                        act.wait_ge(hid_stored[s], stored(h, j, s))
                    act.activation(ebuf[:, s, :], vbuf[:, s, :], ACT.Relu, scale=-1.0).then_inc(neg_done, 1)
                    act.wait_ge(neg_done, g + 1)
                    act.activation(ebuf[:, s, :], ebuf[:, s, :], ACT.Exp, scale=-1.0).then_inc(ex_done, 1)
                    if last and h + 1 < H:
                        split_x(h + 1, 2, 0)
                        act_exp(act, g + 3, 1 - s, prow)
                    if h + 1 < H and not (isinstance(j, int) and j >= KD):
                        split_w1_of(h + 1, j)
                    if h + 1 < H and isinstance(j, int) and j in (KD, KD + 1):
                        split_x(h + 1, j - KD, s)
                    if h == H - 1 and isinstance(j, int):
                        for c in w2_early(j):
                            split_w2(c)
                        if j == NB - 2:
                            split_hT(0, 0, 0)
                    if more(4) and not last:
                        act.wait_ge(t_done, g + 3)
                        scores(nxt(4)[0], nxt(4)[1], s)

                def stored(h, j, s):
                    return 16 * (NB // 2) * h + 8 * (j - s)

                def split_w1_of(h1, k):
                    if isinstance(k, int) and k == 0:
                        act.wait_ge(ld_w1, 16 * (h1 + 1))
                        act.wait_ge(mm_done, 2 * NB * (h1 - 1) + NB)
                    split_w1(k)
                steps(act, NB, 2, 4, step)
                if h + 1 < H:
                    def make(j, s):
                        if not (isinstance(j, int) and (j == 0 or j >= NB - 2)):
                            split_x(h + 1, j + 2, s)
                        split_h(h + 1, j, s)
                    steps(act, NB, 2, 2, make)
                    act_split(act, NB * (h + 1) + 1, 1, PThi)
                    scores(h + 1, 3, 1)

            def h2_out(b, s):
                act.wait_ge(h2_ps, 2 * b + 2)
                act.activation(h2f[:, bass.ds(b, 1), :].rearrange("p o (a n) -> p (o a) n", a=2),
                               h2_banks(s), ACT.Copy).then_inc(h2_sb, 1)

            split_hT(1, 0, 1)
            act.wait_ge(mm_done, 2 * H * NB)
            for c in range(W2E, KC):
                split_w2(c)
            for i in range(2):
                act.wait_ge(hid_stored[i], 16 * H * NB // 2)

            def h2_step(b, s):
                split_hT(2 * b + 2, b + 1, 0)
                split_hT(2 * b + 3, b + 1, 1)
                h2_out(b, s)
            def last_block(b, s):
                act.wait_ge(bc2_ps, 1)
                act.activation(arow2[:, 0:2 * CW].rearrange("p (a n) -> p a n", a=2), PS[0:B, 5:7, 0:CW], ACT.Copy
                               ).then_inc(bc2_sb, 1)
                h2_out(b, s)
            steps(act, NB, 2, 2, lambda b, s: h2_step(b, s) if not (isinstance(b, int) and b == NB - 1) else last_block(b, s))

            act.wait_ge(h2_ps, 2 * NB)
            act.wait_ge(h2_sb, NB)

            def split_h2(b, s):
                act.activation(h2hi[:, bass.ds(b, 1), :], h2f[:, bass.ds(b, 1), :], ACT.Copy).then_inc(h2_hi, 1)

            G2 = H * NB

            def scores2(b, s):
                act_relu(act, s, prow2, arow2[:], al2_up[:, bass.ds(b, 1)])
            split_h2(0, 0)
            act.wait_ge(al2_done, 2 * NB)
            act.activation(al2_up[:], al2[:, 1, :], ACT.Copy, scale=UP).then_inc(up_sb, 1)
            act.wait_ge(bc2_ps, 2)
            act.activation(arow2[:, 2 * CW:N], count_bank(1, 2), ACT.Copy).then_inc(bc2_sb, 1)
            act.wait_ge(up_sb, 2)
            act.wait_ge(bc2_sb, 2)
            scores2(0, 0)
            scores2(1, 1)
            act_exp(act, G2, 0, prow2)
            act_exp(act, G2 + 1, 1, prow2)
            split_h2(1, 1)
            act_split(act, G2, 0, PT2hi)
            with act.Fori(1, NB // 2) as k:
                for u in range(2):
                    split_h2(2 * k + u, u)
            scores2(2, 0)
            act_split(act, G2 + 1, 1, PT2hi)
            scores2(3, 1)
            act_exp(act, G2 + 2, 0, prow2)

            def step2(j, s):
                g = G2 + j
                more = lambda n: not (isinstance(j, int) and j + n >= NB)
                if more(3):
                    act_exp(act, g + 3, 1 - s, prow2)
                if more(2):
                    act.wait_ge(mm2_done, j + 1)
                    act_split(act, g + 2, s, PT2hi)
                if more(4):
                    act.wait_ge(t_done, g + 3)
                    scores2(j + 4, s)
            steps(act, NB, 0, 4, step2)

        @block.vector
        def _(dve):
            dve.memset(mhalf[:], -0.5).then_inc(consts_v, 1)
            dve.memset(ones1[:], 1.0).then_inc(consts_v, 1)
            dve.memset(ecol[:, :, PAIRS:], -1.0).then_inc(consts_v, 1)
            dve.wait_ge(ld_edges, 32)
            dve.tensor_copy(dst_f[:], dst_i[:]).then_inc(edges_f, 1)
            dve.tensor_copy(src_f[:], src_i[:]).then_inc(edges_f, 1)
            dve.wait_ge(edges_f, 1)
            dve.tensor_reduce(dmin[:], dst_f[:].rearrange("p u e -> p (u e)"), AX.X, ALU.min).then_inc(plan, 1)
            dve.tensor_reduce(dmax[:], dst_f[:].rearrange("p u e -> p (u e)"), AX.X, ALU.max).then_inc(plan, 1)
            dve.wait_ge(consts, 8)
            dve.wait_ge(plan, 2)
            dve.tensor_scalar(hit[:, 0, :], blk_hi[:], dmin[:], None, ALU.is_gt)
            dve.tensor_scalar(hit[:, 1, :], blk_lo[:], dmax[:], None, ALU.is_le).then_inc(plan, 1)
            dve.wait_ge(plan, 3)
            dve.tensor_tensor(hit[:, 2, :], hit[:, 0, :], hit[:, 1, :], ALU.mult).then_inc(plan, 1)
            dve.wait_ge(plan, 4)
            dve.tensor_scalar(key[:, 0:NB], hit[:, 2, :], pairid[:], None, ALU.mult).then_inc(plan, 1)
            dve.tensor_scalar(key[:, NB:2 * NB], hit[:, 2, :], pairrv[:], None, ALU.mult).then_inc(plan, 1)
            dve.tensor_copy(ident_b[:], ident[:]).then_inc(consts_v, 1)
            dve.wait_ge(ecol_ps, 1)
            dve.tensor_copy(ecol[:, :, 0:PAIRS], PS[0:B, 7, 0:4 * PAIRS].rearrange("p (a n) -> p a n", a=4)
                            ).then_inc(ecol_sb, 1)
            dve.wait_ge(keys_red, 1)
            dve.tensor_scalar(rng_f[:, 3, :], keyr[0:1, NB:2 * NB], -1.0, float(PAIRS), ALU.mult, ALU.add
                              ).then_inc(plan, 1)
            dve.wait_ge(plan, 7)
            dve.tensor_tensor(rng_f[:, 1, :], keyr[0:1, 0:NB], rng_f[:, 3, :], ALU.subtract)
            dve.tensor_scalar(rng_f[:, 0, :], rng_f[:, 3, :], float(PAIRS - 1), None, ALU.min).then_inc(plan, 1)
            dve.wait_ge(plan, 8)
            dve.tensor_scalar(rng_f[:, 1, :], rng_f[:, 1, :], 1.0, 1.0 / GP, ALU.max, ALU.mult).then_inc(plan, 1)
            dve.wait_ge(plan, 9)
            dve.tensor_scalar(rng_f[:, 1, :], rng_f[:, 1, :], (GP - 1) / (2 * GP), None, ALU.add).then_inc(plan, 1)
            dve.wait_ge(plan, 10)
            dve.tensor_scalar(rng_f[:, 1, :], rng_f[:, 1, :], 2.0 ** 23, None, ALU.add).then_inc(plan, 1)
            dve.wait_ge(plan, 11)
            dve.tensor_scalar(rng_f[:, 1, :], rng_f[:, 1, :], -2.0 ** 23, None, ALU.add).then_inc(plan, 1)
            dve.wait_ge(plan, 12)
            dve.wait_ge(consts_v, 4)
            dve.tensor_tensor_scan(rng_f[:, 3, :], ones1[:], rng_f[:, 1, :], 0.0, ALU.mult, ALU.add
                                   ).then_inc(plan, 1)
            dve.wait_ge(plan, 13)
            dve.tensor_tensor(rng_f[:, 2, :], rng_f[:, 3, :], rng_f[:, 1, :], ALU.subtract)
            dve.tensor_scalar(rng_f[:, 4, :], rng_f[:, 3, :], float(SLOTS), float(DSLOTS), ALU.mult, ALU.add
                              ).then_inc(plan, 1)
            dve.wait_ge(plan, 14)
            dve.tensor_copy(rng_i[:], rng_f[:]).then_inc(ranges, 1)

            def split_xT(j):
                dve.wait_ge(xt_raw_done, j + 1)
                raw = xt_raw[:, j % XR, :].rearrange("p (k n) -> p k n", k=KD)
                dve.tensor_copy(xahi[:, :, j, :], raw).then_inc(xt_hi, 1)
                dve.wait_ge(xt_hi, j + 1)
                dve.tensor_tensor(xalo[:, :, j, :], raw, xahi[:, :, j, :].bitcast(F32), ALU.subtract).then_inc(xt_lo, 1)

            def split_h(h, j, s):
                dve.wait_ge(h_hi, NB * h + j + 1)
                dve.tensor_tensor(hlo[:, bass.ds(j, 1), :].rearrange("p o c -> p (o c)"), PS[0:B, s, :],
                                  hhi[:, bass.ds(j, 1), :].bitcast(F32).rearrange("p o c -> p (o c)"),
                                  ALU.subtract).then_inc(h_lo, 1)

            def fold(n):
                k, half = n // 2, n % 2
                if n == 0:
                    dve.wait_ge(ld_att, 32)
                dve.wait_ge(ld_wk[n % 3], 16 * (n // 3 + 1))
                for i, v in enumerate((2 * half, H + 2 * half, 2 * half + 1, H + 2 * half + 1)):
                    if 4 * n + i >= 2:
                        dve.wait_ge(wa_done, 4 * n + i - 1)
                    dve.tensor_tensor_reduce(out=junk_w[:, i % 2, :], in0=w1raw[:, 2 * (n % 3) + i // 2, :],
                                             in1=attr[:, v, :], scale=1.0, scalar=0.0, op0=ALU.mult, op1=ALU.add,
                                             accum_out=wa_f[:, k, v:v + 1]).then_inc(wa_done, 1)

            def one_hots(b):
                first, count, before = edge_steps(dve, b)
                with dve.Fori(0, count) as i:
                    for v in range(GP):
                        pair = at_pair(first, i, v)
                        dve.wait_ge(oh_free, SLOTS * (before + i) + 2 * v + 2 + DSLOTS - SLOTS)
                        for u in range(2):
                            oh = dve.tensor_scalar(oh_src[:, 2 * v + u, :], colid[:], ecol[:, 2 + u, bass.ds(pair, 1)], None,
                                                   ALU.is_equal)
                        oh.then_inc(oh_done, 1)

            dve.wait_ge(ranges, 1)
            dve.wait_ge(ecol_sb, 1)
            made = []
            for what, b in PROLOGUE:
                if what == "counts":
                    one_hots(b)
                    while made:
                        j = made.pop(0)
                        split_h(0, j, j % 2)
                    if 1 <= b <= 2:
                        for j in range(NB // 2 * (b - 1), NB // 2 * b):
                            split_xT(j)
                elif what == "h":
                    made.append(b)
                elif what == "fold":
                    fold(b)
                    if b == 2 * KD - 1:
                        dve.wait_ge(wa_hi, 1)
                        dve.tensor_tensor(walo[:], wa_f[:], wahi[:].bitcast(F32), ALU.subtract).then_inc(wa_lo, 1)

            def maxima(h, b):
                dve_max(dve, NB * h + b, b, arow[:, H - 1 - h, :], nbr, al[:, H + h, bass.ds(b, 1)])

            dve.wait_ge(al_sb, 1)
            dve.wait_ge(bc_sb, 1)
            dve.wait_ge(c_done, 4)
            maxima(0, 0)
            maxima(0, 1)
            split_h(0, NB - 2, 0)
            split_h(0, NB - 1, 1)
            dve_counts(dve, 0, 0, 0, prow)
            dve_counts(dve, 1, 1, 1, prow)
            maxima(0, 2)
            dve_split(dve, 0, 0, PThi, PTlo)
            maxima(0, 3)
            dve_counts(dve, 2, 2, 0, prow)
            dve_split(dve, 1, 1, PThi, PTlo)
            dve.wait_ge(c_done, NB)
            dve.wait_ge(bc_sb, H)
            dve.wait_ge(ld_b1, 16)

            def split_hT(n, half):
                dve.wait_ge(ht_hi, n + 1)
                for a, bank in enumerate(ht_banks(half)):
                    lo = dve.tensor_tensor(ht_part(half, 1, a), PS[:, bank, 0:4 * B], ht_part(half, 0, a).bitcast(F32),
                                           ALU.subtract)
                lo.then_inc(ht_lo, 1)

            for h in range(H):
                def step(j, s):
                    g = NB * h + j
                    more = lambda n: not (h == H - 1 and isinstance(j, int) and j + n >= NB)
                    at = lambda n: j + n - NB if isinstance(j, int) and j + n >= NB else j + n
                    dve.wait_ge(mm_done, 2 * NB * h + NB + j + 1)
                    dve.wait_ge(d_done, g + 1)
                    dve.scalar_tensor_tensor(vbuf[:, s, :], PS[0:B, s, :], rden[:, bass.ds(g, 1)],
                                             b1row[:, h * HC:(h + 1) * HC], ALU.mult, ALU.add).then_inc(v_done, 1)
                    if h == 0 and not isinstance(j, int):
                        maxima(0, j + 4)
                    if h + 1 < H and isinstance(j, int) and 6 <= j < 9:
                        maxima(h + 1, j - 6)
                    if more(3):
                        dve_counts(dve, g + 3, at(3), 1 - s, prow)
                    last = isinstance(j, int) and j == NB - 1
                    if more(2) and not last:
                        dve_split(dve, g + 2, s, PThi, PTlo)
                    if h == H - 1 and isinstance(j, int) and j == NB - 2:
                        split_hT(0, 0)
                    dve.wait_ge(ex_done, g + 1)
                    dve.scalar_tensor_tensor(ebuf[:, s, :], ebuf[:, s, :], -1.0, vbuf[:, s, :], ALU.add, ALU.max
                                             ).then_inc(hid_done, 1)
                steps(dve, NB, 0, 4, step)
                if h + 1 < H:
                    def make(j, s):
                        split_h(h + 1, j, s)
                        if not (isinstance(j, int) and j >= NB - 3):
                            maxima(h + 1, j + 3)
                    steps(dve, NB, 0, 4, make)
                    dve_split(dve, NB * (h + 1) + 1, 1, PThi, PTlo)

            split_hT(1, 1)
            for c in range(W2E, KC):
                dve.wait_ge(w2_hi, c + 1)
                dve.tensor_tensor(W2p[:, c, 1, :], w2_raw(c), W2p[:, c, 0, :].bitcast(F32), ALU.subtract
                                  ).then_inc(w2_lo, 1)
            dve.wait_ge(ld_a2, 32)

            def scores2(b, s):
                dve.wait_ge(h2_sb, b + 1)
                if not (isinstance(b, int) and b == 0):
                    dve.wait_ge(al2_done, 2 * b)
                blk = h2f[:, bass.ds(b, 1), :].rearrange("p o n -> p (o n)")
                for v in range(2):
                    dve.scalar_tensor_tensor(a2junk[:, v, :], blk, 1.0, a2row[:, v, :], ALU.mult, ALU.mult,
                                             accum_out=al2[:, v, bass.ds(b, 1)]).then_inc(al2_done, 1)

            def h2_step(b, s):
                split_hT(2 * b + 2, 0)
                split_hT(2 * b + 3, 1)
                scores2(b, s)
            steps(dve, NB, 2, 2, lambda b, s: h2_step(b, s) if not (isinstance(b, int) and b == NB - 1) else scores2(b, s))

            G2 = H * NB

            def maxima2(b):
                dve_max(dve, G2 + b, b, arow2[:], nbr2, al2[:, 1, bass.ds(b, 1)])

            def split_h2(b, s):
                dve.wait_ge(h2_hi, b + 1)
                dve.tensor_tensor(h2lo[:, bass.ds(b, 1), :], h2f[:, bass.ds(b, 1), :],
                                  h2hi[:, bass.ds(b, 1), :].bitcast(F32), ALU.subtract).then_inc(h2_lo, 1)
            split_h2(0, 0)
            dve.wait_ge(bc2_sb, 2)
            maxima2(0)
            maxima2(1)
            dve_counts(dve, G2, 0, 0, prow2)
            dve_counts(dve, G2 + 1, 1, 1, prow2)
            split_h2(1, 1)
            dve_split(dve, G2, 0, PT2hi, PT2lo)
            with dve.Fori(1, NB // 2) as k:
                for u in range(2):
                    split_h2(2 * k + u, u)
            maxima2(2)
            maxima2(3)
            dve_counts(dve, G2 + 2, 2, 0, prow2)
            dve_split(dve, G2 + 1, 1, PT2hi, PT2lo)
            dve.wait_ge(ld_b2, 16)

            def step2(j, s):
                g = G2 + j
                more = lambda n: not (isinstance(j, int) and j + n >= NB)
                yb = y[:, bass.ds(j, 1), :]
                y2 = yb.rearrange("p o (a n) -> p (o a) n", a=2)
                y1 = yb.rearrange("p o n -> p (o n)")
                banks = PS[0:B, 0:2, 0:DH] if s == 0 else PS[0:B, 5:7, 0:DH]
                dve.wait_ge(mm2_done, j + 1)
                dve.wait_ge(d_done, g + 1)
                dve.wait_ge(xb_done, j + 1)
                dve.scalar_tensor_tensor(y2, banks, rden[:, bass.ds(g, 1)],
                                         xres[:, s, :].rearrange("p (a n) -> p a n", a=2), ALU.mult, ALU.add
                                         ).then_inc(y_b, 1)
                if more(4):
                    maxima2(j + 4)
                if more(3):
                    dve_counts(dve, g + 3, j + 3, 1 - s, prow2)
                if more(2):
                    dve_split(dve, g + 2, s, PT2hi, PT2lo)
                dve.wait_ge(ld_b2, 16)
                dve.wait_ge(y_b, j + 1)
                for a in range(2):
                    last = dve.bn_stats(bnst[:, a, :], y1[:, a * DH:(a + 1) * DH])
                last.then_inc(y_st, 1)
                dve.wait_ge(ld_b2, 16)
                dve.wait_ge(y_st, j + 1)
                dve.bn_aggr(mv[:],
                            bnst[:].rearrange("p a n -> p (a n)")).then_inc(y_mv, 1)
                dve.wait_ge(y_mv, j + 1)
                dve.tensor_scalar(vpe[:], mv[:, 1:2], EPS, None, ALU.add
                                  ).then_inc(y_var, 1)
                dve.wait_ge(y_pow, j + 1)
                dve.tensor_scalar(y1, y1, mv[:, 0:1],
                                  rstd[:, bass.ds(j, 1)], ALU.subtract, ALU.mult).then_inc(y_done, 1)

            steps(dve, NB, 0, 4, step2)

        @block.tensor
        def _(pe):
            pe.wait_ge(consts, 8)
            pe.wait_ge(edges_f, 2)
            for n in range(4):
                t = pe.transpose(PS[0:B, 7, n * PAIRS:(n + 1) * PAIRS], (dst_f, src_f)[n // 2][:, n % 2, :],
                                 ident[0:PAIRS, 0:PAIRS])
            t.then_inc(ecol_ps, 1)

            def transpose_x(j):
                if j % XL == 0:
                    pe.wait_ge(ld_x[j // XL], 16)
                if j == NB // 2:
                    pe.wait_ge(c_done, 1)
                if j >= 2:
                    pe.wait_ge(xt_raw_done, j - 1)
                p = x_banks(j)
                for k in range(KD):
                    t = pe.transpose(PS[:, p + k // 4, (k % 4) * B:(k % 4 + 1) * B],
                                     xall[:, j, k * 128:(k + 1) * 128],
                                     ident[0:B, 0:B])
                t.then_inc(xt_ps, 1)

            def products(dst, parts, start, stop):
                (ahi, alo), (bhi, blo) = parts
                pe.matmul(dst, ahi, bhi, start=start, stop=False)
                pe.matmul(dst, ahi, blo, start=False, stop=False)
                return pe.matmul(dst, alo, bhi, start=False, stop=stop)

            def h_block(j):
                if j == 0:
                    pe.wait_ge(xt_lo, NB)
                    pe.wait_ge(w1_hi, KD)
                    pe.wait_ge(w1_lo, KD)
                if j >= 2:
                    pe.wait_ge(h_lo, j - 1)
                for k in range(KD):
                    t = products(PS[0:B, j % 2, :], ((xahi[:, k, j, :], xalo[:, k, j, :]), (W1hi[:, k, :], W1lo[:, k, :])),
                                 k == 0, k == KD - 1)
                t.then_inc(mm_done, 1)

            def counts(b):
                s = b % 2
                pe.wait_ge(zeroed, b + 1)
                t = pe.matmul(PS[0:B, 2 + 3 * s + b // BB, (b % BB) * B:(b % BB + 1) * B], ident_b[0:B, 0:B],
                              ident_b[0:B, 0:B], start=False, stop=False, skip_group_check=True)
                if b == 0:
                    t.then_inc(oh_free, DSLOTS)
                _, count, before = edge_steps(pe, b)
                with pe.Fori(0, count) as i:
                    turn = (before + i) % 2
                    for v in range(GP):
                        pe.wait_ge(oh_done, GP * (before + i) + v + 1)
                        pe.wait_ge(ohd_done, GP * (before + i) + v + 1)
                        for slot in (2 * v, 2 * v + 1):
                            for c, (lo, hi) in enumerate(TCH):
                                t = pe.matmul(count_bank(s, c),
                                              oh_dst[:, bass.ds(turn, 1), slot, :].rearrange("p o n -> p (o n)"), oh_src[:, slot, lo * B:hi * B],
                                              start=False, stop=False, skip_group_check=True)
                        t.then_inc(oh_free, 2)

            def score_rows(c):
                lo, hi = TCH[c]
                for k in range(KD):
                    t = products(PS[0:2 * H, c % 2, 0:(hi - lo) * B],
                                 ((wahi[:, k, :], walo[:, k, :]), (xahi[:, k, lo:hi, :].rearrange("p b n -> p (b n)"),
                                   xalo[:, k, lo:hi, :].rearrange("p b n -> p (b n)"))),
                                 k == 0, k == KD - 1)
                t.then_inc(rows_ps, 1)

            def spread(col, set_, lo=0, hi=NB):
                for b in range(lo, hi):
                    t = pe.matmul(PS[0:B, 2 + 3 * set_ + b // BB, (b % BB) * B:(b % BB + 1) * B],
                                  col(b).broadcast_to([B, B]), ident[0:B, 0:B], start=True, stop=True)
                return t

            pe.wait_ge(ranges, 1)
            pe.wait_ge(consts_v, 4)
            for what, b in PROLOGUE:
                if what == "counts":
                    counts(b)
                elif what == "x":
                    for j in range(NB // 2 * b, NB // 2 * (b + 1)):
                        transpose_x(j)
                elif what == "h":
                    h_block(b)
                elif what == "scores" and b == 0:
                    pe.wait_ge(h_lo, NB - 2)
                    pe.wait_ge(wa_hi, 1)
                    pe.wait_ge(wa_lo, 1)
                    score_rows(0)
                    score_rows(1)
                elif what == "scores":
                    pe.wait_ge(rows_sb, 2)
                    score_rows(2)
                    pe.wait_ge(rows_sb, 3)
                    for j in range(NB):
                        t = pe.transpose(PS[0:B, 1, 2 * H * j:2 * H * (j + 1)], rows[:, j * B:(j + 1) * B],
                                         ident[0:2 * H, 0:2 * H])
                    t.then_inc(al_ps, 1)
                    pe.wait_ge(al_sb, 1)
                    pe.wait_ge(c_done, NB - 1)
                    spread(lambda b: al[:, 0, b:b + 1], 0).then_inc(bc_ps, 1)
            h_block(NB - 2)
            h_block(NB - 1)
            pe.wait_ge(c_done, NB)
            for h in range(1, H):
                if h >= 2:
                    pe.wait_ge(bc_sb, h - 1)
                spread(lambda b: al[:, h, b:b + 1], h % 2).then_inc(bc_ps, 1)

            pe.wait_ge(bc_sb, 3)
            pe.wait_ge(pc_done, 1)
            pe_transpose(pe, 0, 0, prow)

            def transpose_h(b, s, half):
                if half == 0:
                    pe.wait_ge(ld_hb[s], 8 * (b - s) + 16)
                if not (isinstance(b, int) and b == 0):
                    pe.wait_ge(ht_lo, 2 * b + half - 1)
                for k in range(KH):
                    t = pe.transpose(PS[:, ht_banks(half)[k // 4], (k % 4) * B:(k % 4 + 1) * B],
                                     hblk[:, s, (half * KH + k) * 128:(half * KH + k + 1) * 128], ident[0:B, 0:B])
                t.then_inc(ht_ps, 1)

            for h in range(H):
                def step(j, s):
                    g = NB * h + j
                    if not (h == H - 1 and isinstance(j, int) and j == NB - 1):
                        pe.wait_ge(pc_done, g + 2)
                        pe.wait_ge(pt_lo, g + 1)
                        pe_transpose(pe, g + 1, 1 - s, prow)
                    else:
                        pe.wait_ge(pt_lo, g + 1)
                    if isinstance(j, int) and j < 2:
                        pe.wait_ge(h_lo, NB * (h + 1))
                    else:
                        pe.wait_ge(v_done, g - 1)
                    if h == H - 1 and isinstance(j, int) and j == NB - 1:
                        transpose_h(0, 0, 0)
                    for b in range(NB):
                        t = products(PS[0:B, s, :], ((PThi[:, s, b, :], PTlo[:, s, b, :]), (hhi[:, b, :], hlo[:, b, :])),
                                     b == 0, b == NB - 1)
                    t.then_inc(mm_done, 1)
                steps(pe, NB, 2, 2, step)
                if h + 1 < H:
                    def make(j, s):
                        if isinstance(j, int) and j < 2:
                            pe.wait_ge(w1_lo, KD * (h + 2))
                            pe.wait_ge(v_done, NB * (h + 1) - 1 + j)
                        else:
                            pe.wait_ge(h_lo, NB * (h + 1) + j - 1)
                        pe.wait_ge(xr_lo, NB * h + j + 1)
                        for k in range(KD):
                            t = products(PS[0:B, s, :],
                                         ((xr[:, s, 0, k * B:(k + 1) * B], xr[:, s, 1, k * B:(k + 1) * B]),
                                          (W1hi[:, k, :], W1lo[:, k, :])), k == 0, k == KD - 1)
                        t.then_inc(mm_done, 1)
                    steps(pe, NB, 2, 0, make)

            def mm_half(b, s, half):
                pe.wait_ge(ht_lo, 2 * b + half + 1)
                for k in range(KH):
                    c = half * KH + k
                    if isinstance(b, int) and b == 0:
                        w2_lo_done(pe, c)
                    for a in range(2):
                        t = products(h2_banks(s)[:, a, :],
                                     ((hT[:, half, 0, k, :], hT[:, half, 1, k, :]),
                                      (W2p[:, c, 0, a * DH:(a + 1) * DH], W2p[:, c, 1, a * DH:(a + 1) * DH])),
                                     c == 0, c == KC - 1)
                t.then_inc(h2_ps, 1)

            transpose_h(0, 0, 1)

            def h2_block(b, s):
                if isinstance(b, int) and b < 2:
                    pe.wait_ge(v_done, H * NB - 1 + b)
                else:
                    pe.wait_ge(h2_sb, b - 1)
                mm_half(b, s, 0)
                if not (isinstance(b, int) and b == NB - 1):
                    transpose_h(b + 1, 1 - s, 0)
                else:
                    pe.wait_ge(al2_done, 2 * b)
                    pe.wait_ge(ht_lo, 2 * NB)
                    spread(lambda n: al2[:, 0, n:n + 1], 1, 0, 2 * BB).then_inc(bc2_ps, 1)
                mm_half(b, s, 1)
                if not (isinstance(b, int) and b == NB - 1):
                    transpose_h(b + 1, 1 - s, 1)
            steps(pe, NB, 2, 2, h2_block)
            pe.wait_ge(al2_done, 2 * NB - 1)
            spread(lambda n: al2[:, 0, n:n + 1], 1, 2 * BB, NB).then_inc(bc2_ps, 1)

            G2 = H * NB
            pe.wait_ge(bc2_sb, 2)
            pe.wait_ge(h2_sb, NB)
            pe.wait_ge(pc_done, G2 + 1)
            pe_transpose(pe, G2, 0, prow2)

            def step2(j, s):
                g = G2 + j
                if not (isinstance(j, int) and j == NB - 1):
                    pe.wait_ge(pc_done, g + 2)
                    pe.wait_ge(pt_lo, g + 1)
                    pe_transpose(pe, g + 1, 1 - s, prow2)
                else:
                    pe.wait_ge(pt_lo, g + 1)
                if not (isinstance(j, int) and j < 2):
                    pe.wait_ge(y_b, j - 1)
                for b in range(NB):
                    if isinstance(j, int) and j == 0:
                        pe.wait_ge(h2_lo, b + 1)
                    for a in range(2):
                        t = products(PS[0:B, 5 * s + a, 0:DH],
                                     ((PT2hi[:, s, b, :], PT2lo[:, s, b, :]),
                                      (h2hi[:, b, a * DH:(a + 1) * DH], h2lo[:, b, a * DH:(a + 1) * DH])),
                                     b == 0, b == NB - 1)
                t.then_inc(mm2_done, 1)
            steps(pe, NB, 2, 2, step2)


_INS = ["x", "src", "dst", "L0_gnn_W1", "L0_gnn_att_src1", "L0_gnn_att_dst1", "L0_gnn_b1",
        "L0_gnn_W2", "L0_gnn_att_src2", "L0_gnn_att_dst2", "L0_gnn_b2"]


def kernel(**inputs):
    import numpy as _np
    import concourse.bacc as _bacc
    from concourse import mybir as _mybir
    from concourse.bass_utils import run_bass_kernel_spmd as _run

    nc = _bacc.Bacc("TRN2", target_bir_lowering=False, num_devices=1)
    arrays, args = {}, []
    for name in _INS:
        a = _np.ascontiguousarray(inputs[name])
        arrays[f"in_{name}"] = a
        args.append(nc.dram_tensor(f"in_{name}", a.shape, _mybir.dt.from_np(a.dtype), kind="ExternalInput").ap())
    args.append(nc.dram_tensor("out_0", (N, D), F32, kind="ExternalOutput").ap())
    gat_kernel(nc, *args)
    r = _run(nc, [arrays], core_ids=[0])
    return r.results[0]["out_0"]
```
